# Optimizing a Trainium2 kernel written in Bass

```python
import numpy as np
import jax
import jax.numpy as jnp

def _softmax(x, axis=-1):
    return jax.nn.softmax(x, axis=axis)

def _gelu(x):
    return jax.nn.gelu(x, approximate=True)

def _silu(x):
    return jax.nn.silu(x)

def _sigmoid(x):
    return jax.nn.sigmoid(x)

def _layernorm(x, axis=-1, eps=1e-05):
    m = jnp.mean(x, axis=axis, keepdims=True)
    v = jnp.var(x, axis=axis, keepdims=True)
    return (x - m) / jnp.sqrt(v + eps)

def _scatter_add(tgt, idx, src, axis=0):
    return tgt.at[idx].add(src)

def _segment_sum(src, seg, n):
    return jax.ops.segment_sum(src, seg, n)
kernel_name = 'mk_cond_resid_d1_seqx_r2_c60329'

def setup_inputs(seed: int=0):
    np.random.seed(seed)
    _w = jnp.asarray

    def _rec_inputs():
        import jax
        import jax.numpy as jnp
        _rk = jax.random.key(seed)
        x = -0.0003929 + 0.9999 * jax.random.normal(jax.random.fold_in(_rk, 1), (8, 512, 1024), jnp.float32)
        _lenS = 512 - jax.random.randint(jax.random.fold_in(_rk, 7), (8,), 0, max(1, 512 // 4) + 1, jnp.int32)
        _lenS2 = 512 - jax.random.randint(jax.random.fold_in(_rk, 8), (8,), 0, max(1, 512 // 4) + 1, jnp.int32)
        cond_2048 = 0.00782532 + 1.00527 * jax.random.normal(jax.random.fold_in(_rk, 11), (8, 1024), jnp.float32)
        return (x, cond_2048)
    x, cond_2048 = _rec_inputs()

    def _L0_cond_setup():
        import jax, jax.numpy as jnp
        import numpy as np
        HEADS = 16
        EPS = 1e-06

        def _rms_norm(x, g):
            xf = x.astype(jnp.float32)
            y = xf * jax.lax.rsqrt(jnp.mean(xf * xf, axis=-1, keepdims=True) + EPS)
            return y.astype(x.dtype) * g
        key = jax.random.key(seed)
        ks = jax.random.split(key, 6)
        b, n, dim, emb_dim = (4, 1024, 1024, 1024)
        d_head = dim // HEADS
        return {'x': jax.random.normal(ks[0], (b, n, dim), jnp.float32), 'emb': jax.random.normal(ks[1], (b, 1, emb_dim), jnp.float32), 'W_emb': jax.random.normal(ks[2], (emb_dim, 2 * dim), jnp.float32) * emb_dim ** (-0.5), 'b_emb': jnp.zeros((2 * dim,), jnp.float32), 'g_norm': jnp.ones((dim,), jnp.float32), 'W_qkv': jax.random.normal(ks[3], (dim, 3 * dim), jnp.float32) * dim ** (-0.5), 'g_q': jnp.ones((d_head,), jnp.float32), 'g_k': jnp.ones((d_head,), jnp.float32), 'W_out': jax.random.normal(ks[4], (dim, dim), jnp.float32) * dim ** (-0.5)}
    _L0_cond_all = _L0_cond_setup()
    _L0_cond_in = {k: v for k, v in _L0_cond_all.items() if k in ('W_emb', 'b_emb', 'g_norm', 'W_qkv', 'g_q', 'g_k', 'W_out')}
    del _L0_cond_all
    return {'x': x, 'cond_2048': cond_2048, 'L0_cond_W_emb': _L0_cond_in['W_emb'], 'L0_cond_b_emb': _L0_cond_in['b_emb'], 'L0_cond_g_norm': _L0_cond_in['g_norm'], 'L0_cond_W_qkv': _L0_cond_in['W_qkv'], 'L0_cond_g_q': _L0_cond_in['g_q'], 'L0_cond_g_k': _L0_cond_in['g_k'], 'L0_cond_W_out': _L0_cond_in['W_out']}

def reference(x, cond_2048, L0_cond_W_emb, L0_cond_b_emb, L0_cond_g_norm, L0_cond_W_qkv, L0_cond_g_q, L0_cond_g_k, L0_cond_W_out):
    import jax
    import jax.numpy as jnp

    def _L0_cond_ref(x, emb, W_emb, b_emb, g_norm, W_qkv, g_q, g_k, W_out):
        import jax, jax.numpy as jnp
        import numpy as np
        HEADS = 16
        EPS = 1e-06

        def _rms_norm(x, g):
            xf = x.astype(jnp.float32)
            y = xf * jax.lax.rsqrt(jnp.mean(xf * xf, axis=-1, keepdims=True) + EPS)
            return y.astype(x.dtype) * g
        b, n, dim = x.shape
        h = HEADS
        d = dim // h
        scale_shift = emb @ W_emb + b_emb
        scale, shift = jnp.split(scale_shift, 2, axis=-1)
        xn = _rms_norm(x, g_norm) * (1.0 + scale) + shift
        qkv = xn @ W_qkv
        qkv = qkv.reshape(b, n, 3, h, d)
        q, k, v = jnp.moveaxis(qkv, 2, 0)
        q = jnp.swapaxes(q, 1, 2)
        k = jnp.swapaxes(k, 1, 2)
        v = jnp.swapaxes(v, 1, 2)
        q = _rms_norm(q, g_q)
        k = _rms_norm(k, g_k)
        logits = jnp.einsum('bhqd,bhkd->bhqk', q, k) * d ** (-0.5)
        attn = jax.nn.softmax(logits, axis=-1)
        o = jnp.einsum('bhqk,bhkd->bhqd', attn, v)
        o = jnp.swapaxes(o, 1, 2).reshape(b, n, dim)
        return o + o @ W_out
    x = x + _L0_cond_ref(x, cond_2048[:, None, :], L0_cond_W_emb, L0_cond_b_emb, L0_cond_g_norm, L0_cond_W_qkv, L0_cond_g_q, L0_cond_g_k, L0_cond_W_out)
    return x

_drawn_inputs = setup_inputs


def setup_inputs(seed=0):
    import zlib

    import numpy as np

    out = dict(_drawn_inputs(seed))
    spreads = {'L0_cond_b_emb': (0.0, 0.1),
     'L0_cond_g_norm': (1.0, 0.2),
     'L0_cond_g_q': (1.0, 0.6),
     'L0_cond_g_k': (1.0, 0.6)}
    factors = {}
    for name, (base, spread) in spreads.items():
        noise = np.random.default_rng([zlib.crc32(name.encode()), seed]).standard_normal(out[name].shape)
        drawn = base * np.exp(spread * noise) if base else spread * noise
        out[name] = jnp.asarray(drawn.astype(out[name].dtype))
    for name, factor in factors.items():
        out[name] = (out[name] * factor).astype(out[name].dtype)
    return out
```

```python
from contextlib import ExitStack

import concourse.bass as bass
from concourse import mybir

F32 = mybir.dt.float32
F32R = mybir.dt.float32r
BF16 = mybir.dt.bfloat16
ALU = mybir.AluOpType
ACT = mybir.ActivationFunctionType
AX = mybir.AxisListType

P = 128
B, T, D = 8, 512, 1024
H, DH = 16, 64
PAIRS = H // 2
KT = D // P
TT = T // P
QKV = 3 * P
EPS = 1e-6
OUT_COLS = [(0, 384), (384, 384), (768, 256)]
NOUT = len(OUT_COLS)


JOBS = PAIRS + NOUT
FLIP_X = 2 * TT
FLIP_PAIR = 2 + 2 * TT
FLIP_BATCH = FLIP_X + PAIRS * FLIP_PAIR
CREDIT = 2

STEPS = """V T0 T1 C0 C1 S0 C2 S1 N0 C3 D0 S2 N1 C4 S3 N2 M0 C5 N3 C6 F0 S4 C7 D1 F1 W0 S5 N4 C8 M1
F2 W1 S6 N5 C9 F3 W2 S7 N6 C10 W3 C11 D2 N7 O0 C12 F4 L0 M2 C13 F5 W4 L1 C14 F6 W5 L2 C15 D3 F7 W6 L3 M3 W7 O1 Q""".split()
STEPS_LAST = """B A0 A1 V T0 T1 S0 X0 S1 N0 A2 X1 S2 N1 A3 S3 N2 X2 N3 C0 C1 X3 C2 C3 D0 F0 S4 C4 F1 W0 M0 S5 N4
C5 C6 F2 W1 S6 N5 C7 D1 F3 W2 S7 N6 C8 M1 C9 W3 C10 C11 D2 N7 O0 F4 C12 L0 M2 F5 W4 C13 L1 F6 W5 C14 L2 C15 D3 F7 W6 L3 M3 W7 O1 Q""".split()


def cond_attention(nc, x, cond_t, w_emb, b_emb, g_norm, w_qkv, g_q, g_k, w_out, out):
    x_rows = x.rearrange("b (t p) d -> b t p d", p=P)
    out_rows = out.rearrange("b (t p) d -> b t p d", p=P)
    w_pair = w_qkv.rearrange("a (k p) n -> a p k n", p=P)

    with ExitStack() as ctx:
        def sb(name, shape, dt=F32):
            return ctx.enter_context(nc.sbuf_tensor(name, shape, dt))

        def sem(name):
            return ctx.enter_context(nc.semaphore(name))

        def bank(name):
            return ctx.enter_context(nc.psum_tensor(name, [P, 512], F32))

        proj_bank = [bank(f"proj_bank{i}") for i in range(2)]
        score_bank = [bank(f"score_bank{i}") for i in range(2)]
        flip_bank = [bank(f"flip_bank{i}") for i in range(2)]
        pv_bank = [bank(f"pv_bank{i}") for i in range(2)]

        w_raw = sb("w_raw", [P, KT, QKV])
        w_split = sb("w_split", [P, KT, 2, QKV], F32R)
        wo_raw = sb("wo_raw", [P, KT, D])
        xn_hi = sb("xn_hi", [P, KT, T], F32R)
        xn_lo = sb("xn_lo", [P, KT, T], F32R)
        o_hi = sb("o_hi", [P, PAIRS, T], F32R)
        o_lo = sb("o_lo", [P, PAIRS, T], F32R)
        qk_stage = sb("qk_stage", [P, TT, 2 * P])
        v_stage = sb("v_stage", [P, TT, P])
        q_split = [sb(f"q_split{h}", [P, T], F32R) for h in range(2)]
        k_hi = [sb(f"k_hi{h}", [P, T], F32R) for h in range(2)]
        k_lo = [sb(f"k_lo{h}", [P, T], F32R) for h in range(2)]
        v_split = sb("v_split", [P, TT, 2 * P], F32R)
        probs = [sb(f"probs{h}", [P, TT, T]) for h in range(2)]
        pt_hi = [sb(f"pt_hi{i}", [P, T], F32R) for i in range(2)]
        pt_lo = [sb(f"pt_lo{i}", [P, T], F32R) for i in range(2)]
        x_tile = [sb(f"x_tile{i}", [P, D]) for i in range(2)]
        y_half = [sb(f"y_half{i}", [P, 512]) for i in range(2)]
        square_out = sb("square_out", [P, D], BF16)
        sq = [sb(f"sq{i}", [P, 2 * P]) for i in range(2)]
        o_part = sb("o_part", [P, T])
        o_pair = sb("o_pair", [P, T])
        NRES = 3
        res = [sb(f"res{i}", [P, 384]) for i in range(NRES)]
        ident = sb("ident", [P, P])
        neg_half = sb("neg_half", [P, 4])
        cond_sb = sb("cond_sb", [P, KT, B])
        b_col = sb("b_col", [P, 2 * KT])
        g_col = sb("g_col", [P, KT])
        gq_raw = sb("gq_raw", [P, 1])
        gq_col = sb("gq_col", [P, 1])
        gk_col = sb("gk_col", [P, 1])
        mod_t = sb("mod_t", [P, 2 * KT, B])
        mod = sb("mod", [P, B, 2 * KT])
        mod_now = sb("mod_now", [P, 2 * KT])
        x_ms = [sb(f"x_ms{i}", [P, 1]) for i in range(2)]
        x_ms_eps = [sb(f"x_ms_eps{i}", [P, 1]) for i in range(2)]
        x_rstd = [sb(f"x_rstd{i}", [P, 1]) for i in range(2)]
        qk_ms = sb("qk_ms", [P, TT, 4])
        qk_ms_eps = sb("qk_ms_eps", [P, TT, 4])
        qk_rstd = sb("qk_rstd", [P, TT, 4])
        neg_max = sb("neg_max", [P, 8])
        row_sum = sb("row_sum", [P, 8])
        row_inv = sb("row_inv", [P, 8])
        emb_tile = probs
        mod_rows = probs[0][0:B, :, :]

        const_loaded = sem("const_loaded")
        emb_loaded = [sem(f"emb_loaded{i}") for i in range(2)]
        emb_used = sem("emb_used")
        emb_done = sem("emb_done")
        ident_zero = sem("ident_zero")
        ident_ready = sem("ident_ready")
        mod_rows_ready = sem("mod_rows_ready")
        mod_turned = sem("mod_turned")
        mod_step = sem("mod_step")
        wo_loaded = sem("wo_loaded")
        wo_ready = sem("wo_ready")
        raw_loaded = [sem(f"raw_loaded{i}") for i in range(2)]
        w_hi_done = sem("w_hi_done")
        w_lo_even = sem("w_lo_even")
        w_lo_odd = sem("w_lo_odd")
        w_used = sem("w_used")
        x_loaded = [sem(f"x_loaded{i}") for i in range(2)]
        x_squared = sem("x_squared")
        x_ms_done = sem("x_ms_done")
        x_rstd_done = sem("x_rstd_done")
        x_scaled = sem("x_scaled")
        mod_now_done = sem("mod_now_done")
        xn_hi_done = sem("xn_hi_done")
        xn_lo_done = sem("xn_lo_done")
        proj_done = sem("proj_done")
        proj_drained = sem("proj_drained")
        v_staged = sem("v_staged")
        v_hi_done = sem("v_hi_done")
        v_lo_done = sem("v_lo_done")
        sq_done = sem("sq_done")
        qk_ms_done = sem("qk_ms_done")
        qk_eps_done = sem("qk_eps_done")
        qk_rstd_done = sem("qk_rstd_done")
        flip_full = sem("flip_full")
        flip_hi = sem("flip_hi")
        flip_free = sem("flip_free")
        score_full = sem("score_full")
        max_done = sem("max_done")
        exp_done = sem("exp_done")
        inv_done = sem("inv_done")
        probs_ready = sem("probs_ready")
        pv_used = sem("pv_used")
        o_part_done = sem("o_part_done")
        o_sum_done = sem("o_sum_done")
        o_hi_done = sem("o_hi_done")
        o_lo_done = sem("o_lo_done")
        res_loaded = [sem(f"res_loaded{i}") for i in range(NRES)]
        res_stored = [sem(f"res_stored{i}") for i in range(NRES)]

        def pair_no(b, p):
            return b * PAIRS + p

        def flip_no(b, p):
            return b * FLIP_BATCH + p * FLIP_PAIR + FLIP_X

        def job_no(b, p):
            return b * JOBS + p + 1

        def out_job(b, c):
            return b * JOBS + PAIRS + 1 + c

        def f32(ap):
            return ap.bitcast(F32)

        def rows(head):
            return slice(head * DH, head * DH + DH)

        def w_source(job_kind, kt):
            if job_kind == "qkv":
                return w_raw[:, kt, :], QKV
            c0, n = OUT_COLS[job_kind]
            return wo_raw[:, kt, c0:c0 + n], n

        def next_kind(kind):
            return kind + 1 if kind + 1 < NOUT else "qkv"

        def v_cols(hi):
            cols = v_split[:, :, :].rearrange("p t (a c) -> p t a c", c=DH)
            return cols[:, :, 0:4:3, :] if hi else cols[:, :, 1:3, :]

        block = ctx.enter_context(nc.Block())

        @block.tensor
        def _(pe):
            def product(j, tt, piece, n, act_hi, act_lo, wait_bank=True):
                dst = proj_bank[tt % 2][:, 0:n]
                if piece == 0 and wait_bank:
                    pe.wait_ge(proj_drained, j * TT + (tt - 1))
                for kt in (2 * piece, 2 * piece + 1):
                    if tt == 0:
                        pe.wait_ge(w_lo_odd if kt % 2 else w_lo_even, j * (KT // 2) + (kt // 2 + 1))
                    a_hi = act_hi[:, kt, tt * P:(tt + 1) * P]
                    a_lo = act_lo[:, kt, tt * P:(tt + 1) * P]
                    w_hi, w_lo = w_split[:, kt, 0, 0:n], w_split[:, kt, 1, 0:n]
                    nc.tensor.matmul(dst, a_hi, w_hi, start=(kt == 0), stop=False)
                    nc.tensor.matmul(dst, a_hi, w_lo, start=False, stop=False)
                    mm = nc.tensor.matmul(dst, a_lo, w_hi, start=False, stop=(kt == KT - 1))
                    if tt == TT - 1 and kt < KT - 1:
                        mm.then_inc(w_used, 1)
                    if kt == KT - 1:
                        mm.then_inc(proj_done, 1)

            def turn_x(u, n, r, wait_bank=True):
                for half in range(2):
                    if wait_bank or r > 0:
                        pe.wait_ge(flip_free, u + (2 * r + half - 1))
                    if half == 0:
                        pe.wait_ge(x_scaled, n + (r + 1))
                    for i in range(4):
                        kt = 4 * half + i
                        mm = nc.tensor.transpose(flip_bank[half][:, i * P:(i + 1) * P],
                                                 x_tile[r % 2][:, kt * P:(kt + 1) * P], ident[:, :])
                    mm.then_inc(flip_full, 1)

            def pair(b, p, steps, next_x):
                it, u0, j = pair_no(b, p), flip_no(b, p), job_no(b, p)
                up = u0 + 2 + (FLIP_X if next_x else 0)
                for step in steps:
                    kind, n = step[0], int(step[1:] or 0)
                    h, i = n // 4, n % 4
                    if kind == "T":
                        pe.wait_ge(flip_free, u0 + (n - 1))
                        if n == 0:
                            pe.wait_ge(proj_drained, j * TT)
                        for tt in range(TT):
                            mm = nc.tensor.transpose(flip_bank[n % 2][:, tt * P:(tt + 1) * P],
                                                     qk_stage[:, tt, n * P:(n + 1) * P], ident[:, :])
                        mm.then_inc(flip_full, 1)
                    elif kind == "X":
                        turn_x(u0 + 2, b * TT + TT, n)
                    elif kind == "C":
                        if next_x and i == 0:
                            pe.wait_ge(xn_lo_done, b * FLIP_X + (FLIP_X + 2 * h + 2))
                        product(j, h, i, QKV, xn_hi, xn_lo)
                    elif kind == "S":
                        pe.wait_ge(exp_done, it * 8 + (n - 2 + 1 + CREDIT))
                        if i == 0:
                            pe.wait_ge(flip_free, u0 + 2)
                        q_t = q_split[h][:, i * P:(i + 1) * P]
                        nc.tensor.matmul(score_bank[n % 2][:, :], q_t, k_hi[h][:, :], start=True, stop=False)
                        nc.tensor.matmul(score_bank[n % 2][:, :], q_t, k_lo[h][:, :], start=False,
                                         stop=True).then_inc(score_full, 1)
                    elif kind == "F":
                        pe.wait_ge(flip_free, up + (n - 1))
                        if i == 0:
                            pe.wait_ge(probs_ready, it * 8 + (4 * h + 4))
                        for qt in range(TT):
                            mm = nc.tensor.transpose(flip_bank[n % 2][:, qt * P:(qt + 1) * P],
                                                     probs[h][:, qt, i * P:(i + 1) * P], ident[:, :])
                        mm.then_inc(flip_full, 1)
                    elif kind == "W":
                        if i == 0:
                            pe.wait_ge(o_sum_done, it * 2 + (h - 1 + CREDIT))
                            pe.wait_ge(v_lo_done, it + 1)
                        pe.wait_ge(flip_free, up + (n + 1))
                        v_t = v_split[:, i, h * P:(h + 1) * P]
                        nc.tensor.matmul(pv_bank[h][:, :], v_t, pt_hi[n % 2][:, :], start=(i == 0), stop=False)
                        nc.tensor.matmul(pv_bank[h][:, :], v_t, pt_lo[n % 2][:, :], start=False,
                                         stop=(i == TT - 1)).then_inc(pv_used, 1)

            def project_out(b):
                pe.wait_ge(o_lo_done, b * PAIRS + (PAIRS + 1))
                for c, (_, n) in enumerate(OUT_COLS):
                    for tt in range(TT):
                        for piece in range(4):
                            product(out_job(b, c), tt, piece, n, o_hi, o_lo)

            pe.sem_inc(pv_used, CREDIT)
            pe.wait_ge(const_loaded, 16 * 5)
            emb_bank = [proj_bank[0], proj_bank[1], score_bank[0], score_bank[1]]
            for kt in range(KT):
                pe.wait_ge(emb_loaded[kt % 2], 16 * (kt // 2 + 1))
                for c in range(4):
                    mm = nc.tensor.matmul(emb_bank[c][0:B, :], cond_sb[:, kt, :], emb_tile[kt % 2][:, c, :],
                                          start=(kt == 0), stop=(kt == KT - 1))
                mm.then_inc(emb_used, 1)
            pe.wait_ge(ident_ready, 1)
            pe.wait_ge(mod_rows_ready, 1)
            for c in range(2 * KT):
                mm = nc.tensor.transpose(pv_bank[0][:, c * B:(c + 1) * B],
                                         mod_rows[:, c // 4, (c % 4) * P:(c % 4 + 1) * P], ident[0:B, 0:B])
            mm.then_inc(mod_turned, 1)
            for r in range(TT):
                turn_x(0, 0, r, wait_bank=False)
            for tt in range(TT):
                pe.wait_ge(xn_lo_done, 2 * tt + 2)
                for piece in range(4):
                    product(0, tt, piece, QKV, xn_hi, xn_lo, wait_bank=tt >= 2)

            with pe.Fori(0, B) as b:
                with pe.Fori(0, PAIRS - 1) as p:
                    pair(b, p, STEPS, False)
                pair(b, PAIRS - 1, STEPS_LAST, True)
                project_out(b)

        @block.scalar
        def _(act):
            def split_hi(j, kind, kt, wait_used=True):
                src, n = w_source(kind, kt)
                if wait_used:
                    if kt < KT - 1:
                        act.wait_ge(w_used, j * (KT - 1) + (kt + 1 - (KT - 1)))
                    else:
                        act.wait_ge(proj_done, j * TT)
                nc.scalar.copy(w_split[:, kt, 0, 0:n], src).then_inc(w_hi_done, 1)

            def square_x(n, r, first=False):
                act.wait_ge(x_loaded[r % 2], n * (2 * 16) + 16 * (r // 2 + 1))
                if not first or r > 0:
                    act.wait_ge(x_squared, n * TT + r)
                nc.scalar.activation(square_out[:, :], x_tile[r % 2][:, :], ACT.Square, scale=D ** -0.5,
                                     accum_out=x_ms[r % 2][:, :]).then_inc(x_squared, 1)

            def xn_high(n, u, r):
                for half in range(2):
                    act.wait_ge(flip_free, u + (2 * r + half + 1))
                    nc.scalar.copy(xn_hi[:, 4 * half:4 * half + 4, r * P:(r + 1) * P],
                                   y_half[half][:, :].rearrange("p (k t) -> p k t", k=4)).then_inc(xn_hi_done, 1)

            def stage_v_square_qk(q, j, tt):
                act.wait_ge(proj_done, j * TT + (tt + 1))
                nc.scalar.copy(v_stage[:, tt, :], proj_bank[tt % 2][:, 2 * P:3 * P]).then_inc(v_staged, 1)
                nc.scalar.activation(sq[tt % 2][:, :], proj_bank[tt % 2][:, 0:2 * P], ACT.Square,
                                     scale=DH ** -0.5).then_inc(sq_done, 1)

            def pair(b, p, steps, next_x):
                it, u0, j = pair_no(b, p), flip_no(b, p), job_no(b, p)
                up = u0 + 2 + (FLIP_X if next_x else 0)
                for step in steps:
                    kind, n = step[0], int(step[1:] or 0)
                    h, i = n // 4, n % 4
                    if kind == "V":
                        act.wait_ge(v_staged, it * TT + TT)
                        act.wait_ge(pv_used, it * 8 + CREDIT)
                        nc.scalar.copy(v_cols(True), v_stage[:, :, :].rearrange("p t (a c) -> p t a c", c=DH)
                                       ).then_inc(v_hi_done, 1)
                    elif kind == "T":
                        act.wait_ge(flip_full, u0 + (n + 1))
                        for head in range(2):
                            mine, other = rows(head), rows(1 - head)
                            if n == 0:
                                op = nc.scalar.activation(q_split[head][mine, :], flip_bank[0][mine, :], ACT.Copy,
                                                          scale=gq_col[mine, :])
                            else:
                                for to in (mine, other):
                                    op = nc.scalar.activation(k_hi[head][to, :], flip_bank[1][mine, :], ACT.Copy,
                                                              scale=gk_col[mine, :])
                        op.then_inc(flip_hi, 1)
                    elif kind == "A":
                        square_x(b + 1, n)
                    elif kind == "X":
                        if n == 0:
                            act.wait_ge(proj_done, j * TT)
                        xn_high(b + 1, u0 + 2, n)
                    elif kind == "S":
                        act.wait_ge(max_done, it * 8 + (n + 1))
                        if i == 0:
                            act.wait_ge(flip_full, u0 + (4 * h - 4))
                        nc.scalar.activation(probs[h][:, i, :], score_bank[n % 2][:, :], ACT.Exp,
                                             bias=neg_max[:, n:n + 1],
                                             accum_out=row_sum[:, n:n + 1]).then_inc(exp_done, 1)
                    elif kind == "F":
                        act.wait_ge(flip_full, up + (n + 1))
                        act.wait_ge(pv_used, it * 8 + (n - 1 + CREDIT))
                        nc.scalar.copy(pt_hi[n % 2][:, :], flip_bank[n % 2][:, :]).then_inc(flip_hi, 1)
                    elif kind == "O":
                        act.wait_ge(pv_used, it * 8 + (4 * n + 4 + CREDIT))
                        act.wait_ge(o_sum_done, it * 2 + (n - 1 + CREDIT))
                        mine, other = rows(n), rows(1 - n)
                        nc.scalar.copy(o_part[mine, :], pv_bank[n][other, :]).then_inc(o_part_done, 1)
                    elif kind == "Q":
                        act.wait_ge(o_sum_done, it * 2 + (2 + CREDIT))
                        nc.scalar.copy(o_hi[:, bass.ds(p, 1), :], o_pair[:, :].unsqueeze(1)).then_inc(o_hi_done, 1)
                    elif kind == "D":
                        if n == 0:
                            act.wait_ge(v_lo_done, it + 1)
                        act.wait_ge(qk_ms_done, it * TT + (TT + n - 1))
                        stage_v_square_qk(it + 1, j, n)
                    elif kind == "L":
                        for kt in (2 * n, 2 * n + 1):
                            split_hi(j + 1, 0 if next_x else "qkv", kt)

            act.sem_inc(exp_done, CREDIT)
            for kt in range(KT):
                act.wait_ge(raw_loaded[kt // 4], 16)
                split_hi(0, "qkv", kt, wait_used=False)
            square_x(0, 0, first=True)
            square_x(0, 1, first=True)
            emb_bank = [proj_bank[0], proj_bank[1], score_bank[0], score_bank[1]]
            act.wait_ge(emb_used, KT)
            for c in range(4):
                cp = nc.scalar.copy(mod_rows[:, c, :], emb_bank[c][0:B, :])
            cp.then_inc(mod_rows_ready, 1)
            xn_high(0, 0, 0)
            square_x(0, 2, first=True)
            xn_high(0, 0, 1)
            square_x(0, 3, first=True)
            xn_high(0, 0, 2)
            xn_high(0, 0, 3)
            for tt in range(TT):
                if tt >= 2:
                    act.wait_ge(qk_ms_done, tt - 1)
                stage_v_square_qk(0, 0, tt)
            for kt in range(KT):
                act.wait_ge(raw_loaded[kt // 4], 32)
                split_hi(1, "qkv", kt)

            with act.Fori(0, B) as b:
                with act.Fori(0, PAIRS - 1) as p:
                    for half in range(2):
                        act.wait_ge(raw_loaded[half], pair_no(b, p) * 16 + 16 * 3)
                    pair(b, p, STEPS, False)
                pair(b, PAIRS - 1, STEPS_LAST, True)
                for c in range(NOUT):
                    nxt = next_kind(c)
                    if nxt == "qkv":
                        for half in range(2):
                            act.wait_ge(raw_loaded[half], b * (PAIRS * 16) + 16 * (PAIRS + 2))
                    for kt in range(KT):
                        split_hi(out_job(b, c) + 1, nxt, kt)

        @block.vector
        def _(dve):
            def split_lo(j, kind, kt):
                src, n = w_source(kind, kt)
                dve.wait_ge(w_hi_done, j * KT + (kt + 1))
                nc.vector.tensor_tensor(w_split[:, kt, 1, 0:n], src, f32(w_split[:, kt, 0, 0:n]),
                                        ALU.subtract).then_inc(w_lo_even, 1)

            def scale_x(n, r):
                dve.wait_ge(x_squared, n + (r + 1))
                nc.vector.tensor_scalar(x_ms_eps[r % 2][:, :], x_ms[r % 2][:, :], EPS, None,
                                        ALU.add).then_inc(x_ms_done, 1)
                dve.wait_ge(x_rstd_done, n + (r + 1))
                nc.vector.tensor_scalar(x_tile[r % 2][:, :], x_tile[r % 2][:, :], x_rstd[r % 2][:, :], None,
                                        ALU.mult).then_inc(x_scaled, 1)

            def modulate(n, u, r, first=False):
                for half in range(2):
                    dve.wait_ge(flip_full, u + (2 * r + half + 1))
                    if not first or r > 0:
                        dve.wait_ge(xn_lo_done, n * 2 + (2 * r + half - 1))
                    for i in range(4):
                        kt = 4 * half + i
                        op = nc.vector.tensor_scalar(y_half[half][:, i * P:(i + 1) * P],
                                                     flip_bank[half][:, i * P:(i + 1) * P],
                                                     mod_now[:, kt:kt + 1], mod_now[:, KT + kt:KT + kt + 1],
                                                     ALU.mult, ALU.add)
                    op.then_inc(flip_free, 1)

            def mean_squares(q, tt):
                dve.wait_ge(sq_done, q + (tt + 1))
                nc.vector.tensor_reduce(qk_ms[:, tt, :], sq[tt % 2][:, :].rearrange("p (h d) -> p h d", d=DH),
                                        AX.X, ALU.add).then_inc(qk_ms_done, 1)
                dve.wait_ge(qk_ms_done, q + (tt + 1))
                nc.vector.tensor_scalar(qk_ms_eps[:, tt, :], qk_ms[:, tt, :], EPS, None,
                                        ALU.add).then_inc(qk_eps_done, 1)

            def stage_qk(q, tt):
                dve.wait_ge(qk_rstd_done, q + (tt + 1))
                nc.vector.tensor_tensor(qk_stage[:, tt, :].rearrange("p (h d) -> p h d", d=DH),
                                        proj_bank[tt % 2][:, 0:2 * P].rearrange("p (h d) -> p h d", d=DH),
                                        qk_rstd[:, tt, :].unsqueeze(2).to_broadcast([P, 4, DH]),
                                        ALU.mult).then_inc(proj_drained, 1)

            def norm_probs(it, n):
                h, i = n // 4, n % 4
                dve.wait_ge(exp_done, it * 8 + (n + 1 + CREDIT))
                nc.vector.reciprocal(row_inv[:, n:n + 1], row_sum[:, n:n + 1]).then_inc(inv_done, 1)
                dve.wait_ge(inv_done, it * 8 + (n + 1))
                nc.vector.tensor_scalar(probs[h][:, i, :], probs[h][:, i, :], row_inv[:, n:n + 1], None,
                                        ALU.mult).then_inc(probs_ready, 1)

            def pair(b, p, steps, next_x):
                it, u0, j = pair_no(b, p), flip_no(b, p), job_no(b, p)
                up = u0 + 2 + (FLIP_X if next_x else 0)
                for step in steps:
                    kind, n = step[0], int(step[1:] or 0)
                    h, i = n // 4, n % 4
                    if kind == "T":
                        dve.wait_ge(flip_hi, it * FLIP_PAIR + (n + 1))
                        for head in range(2):
                            mine, other = rows(head), rows(1 - head)
                            if n == 0:
                                op = nc.vector.scalar_tensor_tensor(
                                    q_split[head][other, :], flip_bank[0][mine, :], gq_col[mine, :],
                                    f32(q_split[head][mine, :]), ALU.mult, ALU.subtract)
                            else:
                                for to in (mine, other):
                                    op = nc.vector.scalar_tensor_tensor(
                                        k_lo[head][to, :], flip_bank[1][mine, :], gk_col[mine, :],
                                        f32(k_hi[head][mine, :]), ALU.mult, ALU.subtract)
                        op.then_inc(flip_free, 1)
                    elif kind == "B":
                        nc.vector.tensor_copy(mod_now[:, :].unsqueeze(1), mod[:, bass.ds((b + 1) % B, 1), :]
                                              ).then_inc(mod_now_done, 1)
                    elif kind == "A":
                        scale_x(b * TT + TT, n)
                    elif kind == "X":
                        if n == 0:
                            dve.wait_ge(mod_now_done, b + 2)
                        modulate(b * TT + TT, u0 + 2, n)
                    elif kind == "S":
                        dve.wait_ge(score_full, it * 8 + (n + 1))
                        nc.vector.tensor_reduce(neg_max[:, n:n + 1], score_bank[n % 2][:, :], AX.X, ALU.max,
                                                negate=True).then_inc(max_done, 1)
                    elif kind == "N":
                        norm_probs(it, n)
                    elif kind == "F":
                        dve.wait_ge(flip_hi, it * FLIP_PAIR + (2 + n + 1))
                        nc.vector.tensor_tensor(pt_lo[n % 2][:, :], flip_bank[n % 2][:, :],
                                                f32(pt_hi[n % 2][:, :]), ALU.subtract).then_inc(flip_free, 1)
                    elif kind == "O":
                        dve.wait_ge(o_part_done, it * 2 + (n + 1))
                        if n == 0:
                            dve.wait_ge(o_lo_done, it + 1)
                        mine = rows(n)
                        nc.vector.tensor_tensor(o_pair[mine, :], pv_bank[n][mine, :], o_part[mine, :],
                                                ALU.add).then_inc(o_sum_done, 1)
                    elif kind == "D":
                        mean_squares(it * TT + TT, n)
                    elif kind == "M":
                        if n == 0:
                            dve.wait_ge(flip_full, u0 + 2)
                        stage_qk(it * TT + TT, n)
                    elif kind == "L":
                        split_lo(j + 1, 0 if next_x else "qkv", 2 * n)

            def add_residual(b, c, tt):
                g = c * TT + tt
                _, n = OUT_COLS[c]
                dve.wait_ge(proj_done, out_job(b, c) * TT + (tt + 1))
                dve.wait_ge(res_loaded[g % NRES], b * (16 * NOUT * TT // NRES) + 16 * (g // NRES + 1))
                nc.vector.tensor_tensor(res[g % NRES][:, 0:n], proj_bank[tt % 2][:, 0:n],
                                        res[g % NRES][:, 0:n], ALU.add).then_inc(proj_drained, 1)

            dve.sem_inc(o_sum_done, CREDIT)
            for kt in range(0, KT, 2):
                split_lo(0, "qkv", kt)
            scale_x(0, 0)
            scale_x(0, 1)
            dve.wait_ge(const_loaded, 16 * 5)
            nc.vector.tensor_scalar(gq_col[:, :], gq_raw[:, :], DH ** -0.5, None, ALU.mult).then_inc(mod_step, 1)
            dve.wait_ge(mod_turned, 1)
            nc.vector.tensor_tensor(mod_t[:, :, :], pv_bank[0][:, 0:2 * KT * B].rearrange("p (c b) -> p c b", b=B),
                                    b_col[:, :].unsqueeze(2).to_broadcast([P, 2 * KT, B]),
                                    ALU.add).then_inc(mod_step, 1)
            dve.wait_ge(mod_step, 2)
            nc.vector.tensor_scalar(mod_t[:, 0:KT, :], mod_t[:, 0:KT, :], 1.0, None, ALU.add).then_inc(mod_step, 1)
            dve.wait_ge(mod_step, 3)
            by_batch = mod[:, :, :].rearrange("p b c -> p c b")
            nc.vector.tensor_tensor(by_batch[:, 0:KT, :], mod_t[:, 0:KT, :],
                                    g_col[:, :].unsqueeze(2).to_broadcast([P, KT, B]),
                                    ALU.mult).then_inc(mod_step, 1)
            nc.vector.tensor_copy(by_batch[:, KT:2 * KT, :], mod_t[:, KT:2 * KT, :]).then_inc(mod_step, 1)
            dve.wait_ge(mod_step, 5)
            nc.vector.tensor_copy(mod_now[:, :], mod[:, 0, :]).then_inc(mod_now_done, 1)
            dve.wait_ge(mod_now_done, 1)
            modulate(0, 0, 0, first=True)
            scale_x(0, 2)
            modulate(0, 0, 1, first=True)
            scale_x(0, 3)
            modulate(0, 0, 2, first=True)
            modulate(0, 0, 3, first=True)
            dve.wait_ge(wo_loaded, 16)
            dve.wait_ge(ident_ready, 1)
            for kt in range(KT):
                d = wo_raw[:, kt, kt * P:(kt + 1) * P]
                op = nc.vector.tensor_tensor(d, d, ident[:, :], ALU.add)
            op.then_inc(wo_ready, 1)
            for tt in range(TT):
                mean_squares(0, tt)
                stage_qk(0, tt)
            for kt in range(0, KT, 2):
                split_lo(1, "qkv", kt)

            with dve.Fori(0, B) as b:
                with dve.Fori(0, PAIRS - 1) as p:
                    pair(b, p, STEPS, False)
                pair(b, PAIRS - 1, STEPS_LAST, True)
                for c in range(NOUT):
                    for tt in range(TT):
                        add_residual(b, c, tt)
                    for kt in range(0, KT, 2):
                        split_lo(out_job(b, c) + 1, next_kind(c), kt)

        @block.gpsimd
        def _(pool):
            def split_lo(j, kind, kt):
                src, n = w_source(kind, kt)
                pool.wait_ge(w_hi_done, j * KT + (kt + 1))
                nc.gpsimd.tensor_tensor(w_split[:, kt, 1, 0:n], src, f32(w_split[:, kt, 0, 0:n]),
                                        ALU.subtract).then_inc(w_lo_odd, 1)

            def rstd_x(n, r):
                pool.wait_ge(x_ms_done, n + (r + 1))
                nc.gpsimd.tensor_tensor(x_rstd[r % 2][:, :], x_ms_eps[r % 2][:, :], neg_half[:, 0:1],
                                        ALU.pow).then_inc(x_rstd_done, 1)

            def rstd_qk(q, tt):
                pool.wait_ge(qk_eps_done, q + (tt + 1))
                nc.gpsimd.tensor_tensor(qk_rstd[:, tt, :], qk_ms_eps[:, tt, :], neg_half[:, :],
                                        ALU.pow).then_inc(qk_rstd_done, 1)

            def xn_low(n, r):
                for half in range(2):
                    pool.wait_ge(xn_hi_done, n + (2 * r + half + 1))
                    cols = slice(4 * half, 4 * half + 4), slice(r * P, (r + 1) * P)
                    nc.gpsimd.tensor_tensor(xn_lo[:, cols[0], cols[1]],
                                            y_half[half][:, :].rearrange("p (k t) -> p k t", k=4),
                                            f32(xn_hi[:, cols[0], cols[1]]),
                                            ALU.subtract).then_inc(xn_lo_done, 1)

            def pair(b, p, steps, next_x):
                it, j = pair_no(b, p), job_no(b, p)
                for step in steps:
                    kind, n = step[0], int(step[1:] or 0)
                    if kind == "V":
                        pool.wait_ge(v_hi_done, it + 1)
                        nc.gpsimd.tensor_tensor(f32r_v_lo(0), v_stage[:, :, 0:DH],
                                                f32(v_split[:, :, 0:DH]), ALU.subtract)
                        nc.gpsimd.tensor_tensor(f32r_v_lo(1), v_stage[:, :, DH:P],
                                                f32(v_split[:, :, 3 * DH:4 * DH]),
                                                ALU.subtract).then_inc(v_lo_done, 1)
                    elif kind == "A":
                        rstd_x(b * TT + TT, n)
                    elif kind == "X":
                        xn_low(b * FLIP_X + FLIP_X, n)
                    elif kind == "Q":
                        pool.wait_ge(o_hi_done, it + 1)
                        nc.gpsimd.tensor_tensor(o_lo[:, bass.ds(p, 1), :], o_pair[:, :].unsqueeze(1),
                                                f32(o_hi[:, bass.ds(p, 1), :]),
                                                ALU.subtract).then_inc(o_lo_done, 1)
                    elif kind == "D":
                        rstd_qk(it * TT + TT, n)
                    elif kind == "L":
                        split_lo(j + 1, 0 if next_x else "qkv", 2 * n + 1)

            def f32r_v_lo(head):
                return v_split[:, :, (1 + head) * DH:(2 + head) * DH]

            pool.sem_inc(o_lo_done, 1)
            nc.gpsimd.memset(neg_half[:, :], -0.5)
            nc.gpsimd.memset(ident[:, :], 0.0).then_inc(ident_zero, 1)
            pool.wait_ge(ident_zero, 1)
            nc.gpsimd.affine_select(out=ident[:, :], in_=ident[:, :], compare_op=ALU.not_equal, fill=1.0, base=0,
                                    pattern=[[-1, P]], channel_multiplier=1).then_inc(ident_ready, 1)
            pool.wait_ge(ident_ready, 1)
            for kt in range(1, KT, 2):
                split_lo(0, "qkv", kt)
            rstd_x(0, 0)
            rstd_x(0, 1)
            xn_low(0, 0)
            rstd_x(0, 2)
            xn_low(0, 1)
            rstd_x(0, 3)
            xn_low(0, 2)
            xn_low(0, 3)
            for tt in range(TT):
                rstd_qk(0, tt)
            for kt in range(1, KT, 2):
                split_lo(1, "qkv", kt)

            with pool.Fori(0, B) as b:
                with pool.Fori(0, PAIRS - 1) as p:
                    pair(b, p, STEPS, False)
                pair(b, PAIRS - 1, STEPS_LAST, True)
                for c in range(NOUT):
                    for kt in range(1, KT, 2):
                        split_lo(out_job(b, c) + 1, next_kind(c), kt)

        def load_res(sp, b, g):
            c, tt = divmod(g, TT)
            c0, n = OUT_COLS[c]
            sp.wait_ge(res_stored[g % NRES], b * (16 * NOUT * TT // NRES) + 16 * (g // NRES + 1))
            sp.dma_start(res[g % NRES][:, 0:n].unsqueeze(1),
                         x_rows[bass.ds(b, 1), tt, :, c0:c0 + n].rearrange("a p d -> p a d")
                         ).then_inc(res_loaded[g % NRES], 16)

        @block.sync
        def _(sp):
            def load_pair(pair_index):
                for half in range(2):
                    kts = slice(4 * half, 4 * half + 4)
                    sp.dma_start(w_raw[:, kts, :].unsqueeze(1),
                                 w_pair[bass.ds(pair_index, 1), :, kts, :].rearrange("a p k n -> p a k n")
                                 ).then_inc(raw_loaded[half], 16)

            def wait_split(j):
                sp.wait_ge(w_lo_even, j * (KT // 2) + KT // 2)
                sp.wait_ge(w_lo_odd, j * (KT // 2) + KT // 2)

            def load_x(nb, r):
                sp.dma_start(x_tile[r % 2][:, :].unsqueeze(1),
                             x_rows[bass.ds(nb, 1), r, :, :].rearrange("a p d -> p a d")
                             ).then_inc(x_loaded[r % 2], 16)

            nc_const = [
                (cond_sb[:, :, :], cond_t),
                (b_col[:, :], b_emb),
                (g_col[:, :], g_norm),
                (gq_raw[0:P, :], g_q.rearrange("(p a) -> p a", a=1)),
                (gk_col[0:P, :], g_k.rearrange("(p a) -> p a", a=1)),
            ]
            for i in range(NRES):
                sp.sem_inc(res_stored[i], 16)
            for dst, src in nc_const:
                sp.dma_start(dst, src).then_inc(const_loaded, 16)
            emb_rows = w_emb.rearrange("(k p) (c n) -> k p c n", p=P, n=512)
            for kt in range(KT):
                if kt >= 2:
                    sp.wait_ge(emb_used, kt - 1)
                sp.dma_start(emb_tile[kt % 2][:, :, :], emb_rows[kt]).then_inc(emb_loaded[kt % 2], 16)
                if kt == 0:
                    load_x(0, 0)
                if kt == 1:
                    load_x(0, 1)
                    load_pair(0)
            wait_split(0)
            load_pair(1)
            for r in range(2, TT):
                sp.wait_ge(xn_lo_done, 2 * (r - 2) + 2)
                load_x(0, r)
            sp.dma_start(wo_raw[:, :, :], w_out.rearrange("(k p) n -> p k n", p=P)).then_inc(wo_loaded, 16)
            wait_split(1)
            load_pair(2)

            with sp.Fori(0, B) as b:
                with sp.Fori(0, PAIRS - 1) as p:
                    wait_split(job_no(b, p) + 1)
                    load_pair((p + 3) % PAIRS)
                for r in range(TT):
                    sp.wait_ge(xn_lo_done, b * FLIP_X + (FLIP_X + 2 * (r - 2) + 2))
                    load_x((b + 1) % B, r)
                for c, (c0, n) in enumerate(OUT_COLS):
                    for tt in range(TT):
                        g = c * TT + tt
                        if g == 0:
                            for early in range(NRES - 1):
                                load_res(sp, b, early)
                        if g + NRES - 1 < NOUT * TT:
                            load_res(sp, b, g + NRES - 1)
                        sp.wait_ge(proj_drained, out_job(b, c) * TT + (tt + 1))
                        sp.dma_start(out_rows[bass.ds(b, 1), tt, :, c0:c0 + n].rearrange("a p d -> p a d"),
                                     res[g % NRES][:, 0:n].unsqueeze(1)).then_inc(res_stored[g % NRES], 16)
                wait_split(out_job(b, NOUT - 1) + 1)
                load_pair(2)
            for i in range(NRES):
                sp.wait_ge(res_stored[i], B * 16 * NOUT * TT // NRES + 16)
            for half in range(2):
                sp.wait_ge(raw_loaded[half], 16 * (B * PAIRS + 3))
            for i in range(2):
                sp.wait_ge(x_loaded[i], 32 * (B + 1))

def kernel(x, cond_2048, L0_cond_W_emb, L0_cond_b_emb, L0_cond_g_norm, L0_cond_W_qkv, L0_cond_g_q, L0_cond_g_k,
           L0_cond_W_out):
    import numpy as np
    import concourse.bacc as bacc
    from concourse.bass_utils import run_bass_kernel_spmd

    w = np.asarray(L0_cond_W_qkv).reshape(D, 3, PAIRS, P).transpose(2, 0, 1, 3).reshape(PAIRS, D, QKV)
    data = {
        "x": np.ascontiguousarray(x),
        "cond_t": np.ascontiguousarray(np.asarray(cond_2048).T.reshape(KT, P, B).transpose(1, 0, 2)),
        "w_emb": np.ascontiguousarray(L0_cond_W_emb),
        "b_emb": np.ascontiguousarray(np.asarray(L0_cond_b_emb).reshape(2 * KT, P).T),
        "g_norm": np.ascontiguousarray(np.asarray(L0_cond_g_norm).reshape(KT, P).T),
        "w_qkv": np.ascontiguousarray(w),
        "g_q": np.concatenate([np.asarray(L0_cond_g_q)] * 2),
        "g_k": np.concatenate([np.asarray(L0_cond_g_k)] * 2),
        "w_out": np.ascontiguousarray(L0_cond_W_out),
    }
    nc = bacc.Bacc("TRN2", target_bir_lowering=False, num_devices=1)
    args = [nc.dram_tensor(f"in_{k}", a.shape, mybir.dt.from_np(a.dtype), kind="ExternalInput").ap()
            for k, a in data.items()]
    out = nc.dram_tensor("out_0", (B, T, D), F32, kind="ExternalOutput").ap()
    cond_attention(nc, *args, out)
    r = run_bass_kernel_spmd(nc, [{f"in_{k}": a for k, a in data.items()}], core_ids=[0])
    return r.results[0]["out_0"]
```

```python
from contextlib import ExitStack

import concourse.bass as bass
from concourse import mybir

F32 = mybir.dt.float32
F32R = mybir.dt.float32r
BF16 = mybir.dt.bfloat16
ALU = mybir.AluOpType
ACT = mybir.ActivationFunctionType
AX = mybir.AxisListType

P = 128
B, T, D = 8, 512, 1024
H, DH = 16, 64
PAIRS = H // 2
KT = D // P
TT = T // P
QKV = 3 * P
EPS = 1e-6
OUT_COLS = [(0, 384), (384, 384), (768, 256)]
NOUT = len(OUT_COLS)


JOBS = PAIRS + NOUT
FLIP_X = 2 * TT
FLIP_PAIR = 2 + 2 * TT
FLIP_BATCH = FLIP_X + PAIRS * FLIP_PAIR
CREDIT = 2

STEPS = """f0 f1 w0 T0 T1 C0 f2 w1 V0 C1 f3 w2 C2 w3 o1 C3 D0 S0 q0 V1 C4 M0 S1 N0 C5 S2 N1 C6 S3 N2 C7 D1 N3 S4 C8 M1
F0 S5 N4 C9 F1 W0 S6 N5 C10 F2 W1 C11 D2 S7 N6 F3 W2 C12 M2 L0 N7 W3 O0 C13 L1 C14 L2 C15 D3 L3 M3""".split()
STEPS_FIRST = """T0 T1 V0 V1 C0 C1 C2 C3 D0 C4 M0 S0 C5 S1 N0 C6 S2 N1 C7 D1 S3 N2 N3 S4 C8 M1
F0 S5 N4 C9 F1 W0 S6 N5 C10 F2 W1 C11 D2 S7 N6 F3 W2 C12 M2 L0 N7 W3 O0 C13 L1 C14 L2 C15 D3 L3 M3""".split()
STEPS_X = """B0 A0 f0 f1 w0 T0 T1 C0 f2 w1 V0 C1 f3 w2 C2 w3 o1 C3 D0 S0 q0 V1 C4 X0 M0 S1 N0 C5 A1 S2 N1 C6 S3 N2 C7 D1 N3 S4 C8 X1 M1
F0 S5 N4 C9 F1 W0 S6 N5 A2 C10 F2 W1 C11 D2 S7 N6 X2 F3 W2 C12 M2 L0 N7 W3 O0 C13 A3 L1 C14 L2 C15 D3 L3 M3 X3""".split()
STEPS_LAST = """f0 f1 w0 T0 T1 C0 f2 w1 V0 C1 f3 w2 C2 w3 o1 C3 D0 S0 q0 V1 C4 M0 S1 N0 S2 N1 C5 S3 N2 C6 N3 S4 C7 D1 F0 S5 N4 M1
F1 W0 C8 S6 N5 F2 W1 C9 S7 N6 F3 W2 C10 N7 W3 O0 F4 C11 D2 F5 W4 C12 M2 L0 F6 W5 C13 L1 F7 W6 C14 L2 W7 O1 Q0
C15 D3 L3 M3""".split()


def flip_places(steps):
    places, u, v = {}, 0, 0
    for step in steps:
        if step[0] in "TFfX":
            places[step] = u, v
            u, v = u + (2 if step[0] == "X" else 1), v + (step[0] != "X")
    return places


def cond_attention(nc, x, cond_t, w_emb, b_emb, g_norm, w_qkv, g_q, g_k, w_out, out):
    x_rows = x.rearrange("b (t p) d -> b t p d", p=P)
    out_rows = out.rearrange("b (t p) d -> b t p d", p=P)
    w_pair = w_qkv.rearrange("a (k p) n -> a p k n", p=P)

    with ExitStack() as ctx:
        def sb(name, shape, dt=F32):
            return ctx.enter_context(nc.sbuf_tensor(name, shape, dt))

        def sem(name):
            return ctx.enter_context(nc.semaphore(name))

        def bank(name):
            return ctx.enter_context(nc.psum_tensor(name, [P, 512], F32))

        proj_bank = [bank(f"proj_bank{i}") for i in range(2)]
        score_bank = [bank(f"score_bank{i}") for i in range(2)]
        flip_bank = [bank(f"flip_bank{i}") for i in range(2)]
        pv_bank = [bank(f"pv_bank{i}") for i in range(2)]

        w_raw = sb("w_raw", [P, KT, QKV])
        w_split = sb("w_split", [P, KT, 2, QKV], F32R)
        wo_raw = sb("wo_raw", [P, KT, D])
        xn_hi = sb("xn_hi", [P, KT, T], F32R)
        xn_lo = sb("xn_lo", [P, KT, T], F32R)
        o_hi = sb("o_hi", [P, PAIRS, T], F32R)
        o_lo = sb("o_lo", [P, PAIRS, T], F32R)
        qk_stage = sb("qk_stage", [P, TT, 2 * P])
        v_stage = sb("v_stage", [P, 2, TT, P])
        q_split = [sb(f"q_split{h}", [P, T], F32R) for h in range(2)]
        k_hi = [sb(f"k_hi{h}", [P, T], F32R) for h in range(2)]
        k_lo = [sb(f"k_lo{h}", [P, T], F32R) for h in range(2)]
        v_split = [sb(f"v_split{h}", [P, TT, P], F32R) for h in range(2)]
        probs = [sb(f"probs{h}", [P, TT, T]) for h in range(2)]
        pt_hi = [sb(f"pt_hi{i}", [P, T], F32R) for i in range(2)]
        pt_lo = [sb(f"pt_lo{i}", [P, T], F32R) for i in range(2)]
        x_tile = [sb(f"x_tile{i}", [P, D]) for i in range(2)]
        y_half = [sb(f"y_half{i}", [P, 512]) for i in range(2)]
        square_out = sb("square_out", [P, D], BF16)
        sq = [sb(f"sq{i}", [P, 2 * P]) for i in range(2)]
        o_part = sb("o_part", [P, T])
        o_pair = sb("o_pair", [P, T])
        NRES = 3
        res = [sb(f"res{i}", [P, 384]) for i in range(NRES)]
        ident = sb("ident", [P, P])
        neg_half = sb("neg_half", [P, 4])
        cond_sb = sb("cond_sb", [P, KT, B])
        b_col = sb("b_col", [P, 2 * KT])
        g_col = sb("g_col", [P, KT])
        gq_raw = sb("gq_raw", [P, 1])
        gq_col = sb("gq_col", [P, 1])
        gk_col = sb("gk_col", [P, 1])
        mod_t = sb("mod_t", [P, 2 * KT, B])
        mod = sb("mod", [P, B, 2 * KT])
        mod_now = sb("mod_now", [P, 2 * KT])
        x_ms = [sb(f"x_ms{i}", [P, 1]) for i in range(2)]
        x_ms_eps = [sb(f"x_ms_eps{i}", [P, 1]) for i in range(2)]
        x_rstd = [sb(f"x_rstd{i}", [P, 1]) for i in range(2)]
        qk_ms = sb("qk_ms", [P, TT, 4])
        qk_ms_eps = sb("qk_ms_eps", [P, TT, 4])
        qk_rstd = sb("qk_rstd", [P, TT, 4])
        neg_max = sb("neg_max", [P, 8])
        row_sum = sb("row_sum", [P, 8])
        row_inv = sb("row_inv", [P, 8])
        emb_tile = probs
        mod_rows = probs[0][0:B, :, :]

        const_loaded = sem("const_loaded")
        emb_loaded = [sem(f"emb_loaded{i}") for i in range(2)]
        emb_used = sem("emb_used")
        emb_done = sem("emb_done")
        ident_zero = sem("ident_zero")
        ident_ready = sem("ident_ready")
        mod_rows_ready = sem("mod_rows_ready")
        mod_turned = sem("mod_turned")
        mod_step = sem("mod_step")
        wo_loaded = sem("wo_loaded")
        wo_ready = sem("wo_ready")
        raw_loaded = [sem(f"raw_loaded{i}") for i in range(2)]
        w_hi_done = sem("w_hi_done")
        w_lo_even = sem("w_lo_even")
        w_lo_odd = sem("w_lo_odd")
        w_used = sem("w_used")
        x_loaded = [sem(f"x_loaded{i}") for i in range(2)]
        x_squared = sem("x_squared")
        x_ms_done = sem("x_ms_done")
        x_rstd_done = sem("x_rstd_done")
        x_scaled = sem("x_scaled")
        mod_now_done = sem("mod_now_done")
        xn_hi_done = sem("xn_hi_done")
        xn_lo_done = sem("xn_lo_done")
        proj_done = sem("proj_done")
        proj_drained = sem("proj_drained")
        v_staged = sem("v_staged")
        v_hi_done = sem("v_hi_done")
        v_lo_done = sem("v_lo_done")
        sq_done = sem("sq_done")
        qk_ms_done = sem("qk_ms_done")
        qk_eps_done = sem("qk_eps_done")
        qk_rstd_done = sem("qk_rstd_done")
        flip_full = sem("flip_full")
        flip_hi = sem("flip_hi")
        flip_free = sem("flip_free")
        score_full = sem("score_full")
        max_done = sem("max_done")
        exp_done = sem("exp_done")
        inv_done = sem("inv_done")
        probs_ready = sem("probs_ready")
        pv_used = sem("pv_used")
        o_part_done = sem("o_part_done")
        o_sum_done = sem("o_sum_done")
        o_hi_done = sem("o_hi_done")
        o_lo_done = sem("o_lo_done")
        res_loaded = [sem(f"res_loaded{i}") for i in range(NRES)]
        res_stored = [sem(f"res_stored{i}") for i in range(NRES)]

        def pair_no(b, p):
            return b * PAIRS + p

        def turned_before(b, p, batch):
            return b * batch if isinstance(p, int) and p == 0 else b * batch + p * FLIP_PAIR - TT

        def flip_no(b, p):
            last = isinstance(p, int) and p == PAIRS - 1
            return turned_before(b, p, FLIP_BATCH) + (2 * FLIP_X if last else FLIP_X)

        def flip_hi_no(b, p):
            return turned_before(b, p, PAIRS * FLIP_PAIR)

        def job_no(b, p):
            return b * JOBS + p + 1

        def out_job(b, c):
            return b * JOBS + PAIRS + 1 + c

        def f32(ap):
            return ap.bitcast(F32)

        def rows(head):
            return slice(head * DH, head * DH + DH)

        def w_source(job_kind, kt):
            if job_kind == "qkv":
                return w_raw[:, kt, :], QKV
            c0, n = OUT_COLS[job_kind]
            return wo_raw[:, kt, c0:c0 + n], n

        def next_kind(kind):
            return kind + 1 if kind + 1 < NOUT else "qkv"

        def v_part(p, head):
            return v_stage[:, bass.ds(p % 2, 1), :, rows(head)].rearrange("p a t d -> p (a t) d")

        block = ctx.enter_context(nc.Block())

        @block.tensor
        def _(pe):
            def product(j, tt, piece, n, act_hi, act_lo, wait_bank=True):
                dst = proj_bank[tt % 2][:, 0:n]
                if piece == 0 and wait_bank:
                    pe.wait_ge(proj_drained, j * TT + (tt - 1))
                for kt in (2 * piece, 2 * piece + 1):
                    if tt == 0:
                        pe.wait_ge(w_lo_odd if kt % 2 else w_lo_even, j * (KT // 2) + (kt // 2 + 1))
                    a_hi = act_hi[:, kt, tt * P:(tt + 1) * P]
                    a_lo = act_lo[:, kt, tt * P:(tt + 1) * P]
                    w_hi, w_lo = w_split[:, kt, 0, 0:n], w_split[:, kt, 1, 0:n]
                    nc.tensor.matmul(dst, a_hi, w_hi, start=(kt == 0), stop=False)
                    nc.tensor.matmul(dst, a_hi, w_lo, start=False, stop=False)
                    mm = nc.tensor.matmul(dst, a_lo, w_hi, start=False, stop=(kt == KT - 1))
                    if tt == TT - 1 and kt < KT - 1:
                        mm.then_inc(w_used, 1)
                    if kt == KT - 1:
                        mm.then_inc(proj_done, 1)

            def turn_x(u0, u, n, r, wait_bank=True):
                for half in range(2):
                    if wait_bank:
                        pe.wait_ge(flip_free, u0 + (u + half - 1))
                    if half == 0:
                        pe.wait_ge(x_scaled, n + (r + 1))
                    for i in range(4):
                        kt = 4 * half + i
                        mm = nc.tensor.transpose(flip_bank[(u + half) % 2][:, i * P:(i + 1) * P],
                                                 x_tile[r % 2][:, kt * P:(kt + 1) * P], ident[:, :])
                    mm.then_inc(flip_full, 1)

            def pair(b, p, steps, next_x):
                it, u0, j, places = pair_no(b, p), flip_no(b, p), job_no(b, p), flip_places(steps)
                for step in steps:
                    kind, n, pair_of = step[0].upper(), int(step[1:]), it
                    if step[0] in "fw":
                        n, pair_of = n + 4, it - 1
                    if step[0] in "oq":
                        pair_of = it - 1
                    h, i = n // 4, n % 4
                    u, u_hi = places.get(step, (0, 0))
                    if kind == "T":
                        pe.wait_ge(flip_free, u0 + (u - 1))
                        if n == 0:
                            pe.wait_ge(proj_drained, j * TT)
                        for tt in range(TT):
                            mm = nc.tensor.transpose(flip_bank[u % 2][:, tt * P:(tt + 1) * P],
                                                     qk_stage[:, tt, n * P:(n + 1) * P], ident[:, :])
                        mm.then_inc(flip_full, 1)
                    elif kind == "X":
                        turn_x(u0, u, b * TT + TT, n)
                    elif kind == "C":
                        if next_x and i == 0:
                            pe.wait_ge(xn_lo_done, b * FLIP_X + (FLIP_X + 2 * h + 2))
                        product(j, h, i, QKV, xn_hi, xn_lo)
                    elif kind == "S":
                        pe.wait_ge(exp_done, it * 8 + (n - 2 + 1 + CREDIT))
                        if i == 0:
                            pe.wait_ge(flip_free, u0 + (places["T1"][0] + 1))
                        q_t = q_split[h][:, i * P:(i + 1) * P]
                        nc.tensor.matmul(score_bank[n % 2][:, :], q_t, k_hi[h][:, :], start=True, stop=False)
                        nc.tensor.matmul(score_bank[n % 2][:, :], q_t, k_lo[h][:, :], start=False,
                                         stop=True).then_inc(score_full, 1)
                    elif kind == "F":
                        pe.wait_ge(flip_free, u0 + (u - 1))
                        if i == 0:
                            pe.wait_ge(probs_ready, pair_of * 8 + (4 * h + 4))
                        for qt in range(TT):
                            mm = nc.tensor.transpose(flip_bank[u % 2][:, qt * P:(qt + 1) * P],
                                                     probs[h][:, qt, i * P:(i + 1) * P], ident[:, :])
                        mm.then_inc(flip_full, 1)
                    elif kind == "W":
                        if i == 0:
                            pe.wait_ge(o_sum_done, pair_of * 2 + (h - 1 + CREDIT))
                            pe.wait_ge(v_lo_done, pair_of * 2 + (h + 1 + CREDIT))
                        turned = places[("f" if step[0] == "w" else "F") + step[1:]][0]
                        pe.wait_ge(flip_free, u0 + (turned + 1))
                        v_t = v_split[h][:, i, :]
                        nc.tensor.matmul(pv_bank[h][:, :], v_t, pt_hi[n % 2][:, :], start=(i == 0), stop=False)
                        nc.tensor.matmul(pv_bank[h][:, :], v_t, pt_lo[n % 2][:, :], start=False,
                                         stop=(i == TT - 1)).then_inc(pv_used, 1)

            def project_out(b):
                pe.wait_ge(o_lo_done, b * PAIRS + (PAIRS + 1))
                for c, (_, n) in enumerate(OUT_COLS):
                    for tt in range(TT):
                        for piece in range(4):
                            product(out_job(b, c), tt, piece, n, o_hi, o_lo)

            pe.sem_inc(pv_used, CREDIT)
            pe.wait_ge(const_loaded, 16 * 5)
            emb_bank = [proj_bank[0], proj_bank[1], score_bank[0], score_bank[1]]
            for kt in range(KT):
                pe.wait_ge(emb_loaded[kt % 2], 16 * (kt // 2 + 1))
                for c in range(4):
                    mm = nc.tensor.matmul(emb_bank[c][0:B, :], cond_sb[:, kt, :], emb_tile[kt % 2][:, c, :],
                                          start=(kt == 0), stop=(kt == KT - 1))
                mm.then_inc(emb_used, 1)
            pe.wait_ge(ident_ready, 1)
            pe.wait_ge(mod_rows_ready, 1)
            for c in range(2 * KT):
                mm = nc.tensor.transpose(pv_bank[0][:, c * B:(c + 1) * B],
                                         mod_rows[:, c // 4, (c % 4) * P:(c % 4 + 1) * P], ident[0:B, 0:B])
            mm.then_inc(mod_turned, 1)
            for r in range(TT):
                turn_x(0, 2 * r, 0, r, wait_bank=r > 0)
            for tt in range(TT):
                pe.wait_ge(xn_lo_done, 2 * tt + 2)
                for piece in range(4):
                    product(0, tt, piece, QKV, xn_hi, xn_lo, wait_bank=tt >= 2)

            with pe.Fori(0, B) as b:
                pair(b, 0, STEPS_FIRST, False)
                with pe.Fori(1, PAIRS - 2) as p:
                    pair(b, p, STEPS, False)
                pair(b, PAIRS - 2, STEPS_X, False)
                pair(b, PAIRS - 1, STEPS_LAST, True)
                project_out(b)

        @block.scalar
        def _(act):
            def split_hi(j, kind, kt, wait_used=True):
                src, n = w_source(kind, kt)
                if wait_used:
                    if kt < KT - 1:
                        act.wait_ge(w_used, j * (KT - 1) + (kt + 1 - (KT - 1)))
                    else:
                        act.wait_ge(proj_done, j * TT)
                nc.scalar.copy(w_split[:, kt, 0, 0:n], src).then_inc(w_hi_done, 1)

            def square_x(n, r, first=False):
                act.wait_ge(x_loaded[r % 2], n * (2 * 16) + 16 * (r // 2 + 1))
                if not first or r > 0:
                    act.wait_ge(x_squared, n * TT + r)
                nc.scalar.activation(square_out[:, :], x_tile[r % 2][:, :], ACT.Square, scale=D ** -0.5,
                                     accum_out=x_ms[r % 2][:, :]).then_inc(x_squared, 1)

            def xn_high(u0, u, r):
                for half in range(2):
                    act.wait_ge(flip_free, u0 + (u + half + 1))
                    nc.scalar.copy(xn_hi[:, 4 * half:4 * half + 4, r * P:(r + 1) * P],
                                   y_half[half][:, :].rearrange("p (k t) -> p k t", k=4)).then_inc(xn_hi_done, 1)

            def stage_v_square_qk(j, tt, stage):
                act.wait_ge(proj_done, j * TT + (tt + 1))
                nc.scalar.copy(v_stage[:, stage, tt, :], proj_bank[tt % 2][:, 2 * P:3 * P].unsqueeze(1)).then_inc(v_staged, 1)
                nc.scalar.activation(sq[tt % 2][:, :], proj_bank[tt % 2][:, 0:2 * P], ACT.Square,
                                     scale=DH ** -0.5).then_inc(sq_done, 1)

            def pair(b, p, steps, next_x):
                it, u0, j, places = pair_no(b, p), flip_no(b, p), job_no(b, p), flip_places(steps)
                for step in steps:
                    kind, n, pair_of = step[0].upper(), int(step[1:]), it
                    if step[0] in "fw":
                        n, pair_of = n + 4, it - 1
                    if step[0] in "oq":
                        pair_of = it - 1
                    h, i = n // 4, n % 4
                    u, u_hi = places.get(step, (0, 0))
                    if kind == "V":
                        act.wait_ge(v_staged, it * TT + TT)
                        act.wait_ge(pv_used, it * 8 + CREDIT if n == 1 or steps is STEPS_FIRST else it * 8 - 4 + CREDIT)
                        nc.scalar.copy(v_split[n][:, :, rows(n)], v_part(p, n)).then_inc(v_hi_done, 1)
                    elif kind == "T":
                        act.wait_ge(flip_full, u0 + (u + 1))
                        for head in range(2):
                            mine, other = rows(head), rows(1 - head)
                            if n == 0:
                                op = nc.scalar.activation(q_split[head][mine, :], flip_bank[u % 2][mine, :], ACT.Copy,
                                                          scale=gq_col[mine, :])
                            else:
                                for to in (mine, other):
                                    op = nc.scalar.activation(k_hi[head][to, :], flip_bank[u % 2][mine, :], ACT.Copy,
                                                              scale=gk_col[mine, :])
                        op.then_inc(flip_hi, 1)
                    elif kind == "A":
                        square_x(b + 1, n)
                    elif kind == "X":
                        act.wait_ge(proj_done, j * TT + (n + 1))
                        xn_high(u0, u, n)
                    elif kind == "S":
                        act.wait_ge(max_done, it * 8 + (n + 1))
                        if i == 0:
                            act.wait_ge(flip_full, u0 + (places["f3"][0] + 1 if h and "f3" in places else 0))
                        nc.scalar.activation(probs[h][:, i, :], score_bank[n % 2][:, :], ACT.Exp,
                                             bias=neg_max[:, n:n + 1],
                                             accum_out=row_sum[:, n:n + 1]).then_inc(exp_done, 1)
                    elif kind == "F":
                        act.wait_ge(flip_full, u0 + (u + 1))
                        act.wait_ge(pv_used, pair_of * 8 + (n - 1 + CREDIT))
                        nc.scalar.copy(pt_hi[n % 2][:, :], flip_bank[u % 2][:, :]).then_inc(flip_hi, 1)
                    elif kind == "O":
                        act.wait_ge(pv_used, pair_of * 8 + (4 * n + 4 + CREDIT))
                        act.wait_ge(o_sum_done, pair_of * 2 + (n - 1 + CREDIT))
                        mine, other = rows(n), rows(1 - n)
                        nc.scalar.copy(o_part[mine, :], pv_bank[n][other, :]).then_inc(o_part_done, 1)
                    elif kind == "Q":
                        act.wait_ge(o_sum_done, pair_of * 2 + (2 + CREDIT))
                        place = bass.ds(p - 1 if step[0] == "q" else p, 1)
                        nc.scalar.copy(o_hi[:, place, :], o_pair[:, :].unsqueeze(1)).then_inc(o_hi_done, 1)
                    elif kind == "D":
                        if n == 0:
                            act.wait_ge(v_lo_done, it * 2 + CREDIT)
                        act.wait_ge(qk_ms_done, it * TT + (TT + n - 1))
                        stage_v_square_qk(j, n, bass.ds((p + 1) % 2, 1))
                    elif kind == "L":
                        if n % 2 == 0 and not next_x:
                            act.wait_ge(raw_loaded[n // 2], it * 16 + 16 * 3)
                        for kt in (2 * n, 2 * n + 1):
                            split_hi(j + 1, 0 if next_x else "qkv", kt)

            act.sem_inc(exp_done, CREDIT)
            for kt in range(KT):
                act.wait_ge(raw_loaded[kt // 4], 16)
                split_hi(0, "qkv", kt, wait_used=False)
            square_x(0, 0, first=True)
            square_x(0, 1, first=True)
            emb_bank = [proj_bank[0], proj_bank[1], score_bank[0], score_bank[1]]
            act.wait_ge(emb_used, KT)
            for c in range(4):
                cp = nc.scalar.copy(mod_rows[:, c, :], emb_bank[c][0:B, :])
            cp.then_inc(mod_rows_ready, 1)
            xn_high(0, 0, 0)
            square_x(0, 2, first=True)
            xn_high(0, 2, 1)
            square_x(0, 3, first=True)
            xn_high(0, 4, 2)
            xn_high(0, 6, 3)
            for tt in range(TT):
                if tt >= 2:
                    act.wait_ge(qk_ms_done, tt - 1)
                stage_v_square_qk(0, tt, slice(0, 1))
            for kt in range(KT):
                act.wait_ge(raw_loaded[kt // 4], 32)
                split_hi(1, "qkv", kt)

            with act.Fori(0, B) as b:
                pair(b, 0, STEPS_FIRST, False)
                with act.Fori(1, PAIRS - 2) as p:
                    pair(b, p, STEPS, False)
                pair(b, PAIRS - 2, STEPS_X, False)
                pair(b, PAIRS - 1, STEPS_LAST, True)
                for c in range(NOUT):
                    nxt = next_kind(c)
                    for kt in range(KT):
                        if nxt == "qkv" and kt % 4 == 0:
                            act.wait_ge(raw_loaded[kt // 4], b * (PAIRS * 16) + 16 * (PAIRS + 2))
                        split_hi(out_job(b, c) + 1, nxt, kt)

        @block.vector
        def _(dve):
            def split_lo(j, kind, kt):
                src, n = w_source(kind, kt)
                dve.wait_ge(w_hi_done, j * KT + (kt + 1))
                nc.vector.tensor_tensor(w_split[:, kt, 1, 0:n], src, f32(w_split[:, kt, 0, 0:n]),
                                        ALU.subtract).then_inc(w_lo_even, 1)

            def scale_x(n, r):
                dve.wait_ge(x_squared, n + (r + 1))
                nc.vector.tensor_scalar(x_ms_eps[r % 2][:, :], x_ms[r % 2][:, :], EPS, None,
                                        ALU.add).then_inc(x_ms_done, 1)
                dve.wait_ge(x_rstd_done, n + (r + 1))
                nc.vector.tensor_scalar(x_tile[r % 2][:, :], x_tile[r % 2][:, :], x_rstd[r % 2][:, :], None,
                                        ALU.mult).then_inc(x_scaled, 1)

            def modulate(n, u0, u, r, first=False):
                for half in range(2):
                    dve.wait_ge(flip_full, u0 + (u + half + 1))
                    if not first or r > 0:
                        dve.wait_ge(xn_lo_done, n * 2 + (2 * r + half - 1))
                    for i in range(4):
                        kt = 4 * half + i
                        op = nc.vector.tensor_scalar(y_half[half][:, i * P:(i + 1) * P],
                                                     flip_bank[(u + half) % 2][:, i * P:(i + 1) * P],
                                                     mod_now[:, kt:kt + 1], mod_now[:, KT + kt:KT + kt + 1],
                                                     ALU.mult, ALU.add)
                    op.then_inc(flip_free, 1)

            def mean_squares(q, tt):
                dve.wait_ge(sq_done, q + (tt + 1))
                nc.vector.tensor_reduce(qk_ms[:, tt, :], sq[tt % 2][:, :].rearrange("p (h d) -> p h d", d=DH),
                                        AX.X, ALU.add).then_inc(qk_ms_done, 1)
                dve.wait_ge(qk_ms_done, q + (tt + 1))
                nc.vector.tensor_scalar(qk_ms_eps[:, tt, :], qk_ms[:, tt, :], EPS, None,
                                        ALU.add).then_inc(qk_eps_done, 1)

            def stage_qk(q, tt):
                dve.wait_ge(qk_rstd_done, q + (tt + 1))
                nc.vector.tensor_tensor(qk_stage[:, tt, :].rearrange("p (h d) -> p h d", d=DH),
                                        proj_bank[tt % 2][:, 0:2 * P].rearrange("p (h d) -> p h d", d=DH),
                                        qk_rstd[:, tt, :].unsqueeze(2).to_broadcast([P, 4, DH]),
                                        ALU.mult).then_inc(proj_drained, 1)

            def norm_probs(it, n):
                h, i = n // 4, n % 4
                dve.wait_ge(exp_done, it * 8 + (n + 1 + CREDIT))
                nc.vector.reciprocal(row_inv[:, n:n + 1], row_sum[:, n:n + 1]).then_inc(inv_done, 1)
                dve.wait_ge(inv_done, it * 8 + (n + 1))
                nc.vector.tensor_scalar(probs[h][:, i, :], probs[h][:, i, :], row_inv[:, n:n + 1], None,
                                        ALU.mult).then_inc(probs_ready, 1)

            def pair(b, p, steps, next_x):
                it, u0, j, places = pair_no(b, p), flip_no(b, p), job_no(b, p), flip_places(steps)
                for step in steps:
                    kind, n, pair_of = step[0].upper(), int(step[1:]), it
                    if step[0] in "fw":
                        n, pair_of = n + 4, it - 1
                    if step[0] in "oq":
                        pair_of = it - 1
                    h, i = n // 4, n % 4
                    u, u_hi = places.get(step, (0, 0))
                    if kind == "T":
                        dve.wait_ge(flip_hi, flip_hi_no(b, p) + (u_hi + 1))
                        for head in range(2):
                            mine, other = rows(head), rows(1 - head)
                            if n == 0:
                                op = nc.vector.scalar_tensor_tensor(
                                    q_split[head][other, :], flip_bank[u % 2][mine, :], gq_col[mine, :],
                                    f32(q_split[head][mine, :]), ALU.mult, ALU.subtract)
                            else:
                                op = nc.vector.scalar_tensor_tensor(
                                    k_lo[head][mine, :], flip_bank[u % 2][mine, :], gk_col[mine, :],
                                    f32(k_hi[head][mine, :]), ALU.mult, ALU.subtract)
                        op.then_inc(flip_free, 1)
                    elif kind == "B":
                        nc.vector.tensor_copy(mod_now[:, :].unsqueeze(1), mod[:, bass.ds((b + 1) % B, 1), :]
                                              ).then_inc(mod_now_done, 1)
                    elif kind == "A":
                        scale_x(b * TT + TT, n)
                    elif kind == "X":
                        if n == 0:
                            dve.wait_ge(mod_now_done, b + 2)
                        modulate(b * TT + TT, u0, u, n)
                    elif kind == "S":
                        dve.wait_ge(score_full, it * 8 + (n + 1))
                        nc.vector.tensor_reduce(neg_max[:, n:n + 1], score_bank[n % 2][:, :], AX.X, ALU.max,
                                                negate=True).then_inc(max_done, 1)
                    elif kind == "N":
                        norm_probs(it, n)
                    elif kind == "F":
                        dve.wait_ge(flip_hi, flip_hi_no(b, p) + (u_hi + 1))
                        nc.vector.tensor_tensor(pt_lo[n % 2][:, :], flip_bank[u % 2][:, :],
                                                f32(pt_hi[n % 2][:, :]), ALU.subtract).then_inc(flip_free, 1)
                    elif kind == "O":
                        dve.wait_ge(o_part_done, pair_of * 2 + (n + 1))
                        if n == 0:
                            dve.wait_ge(o_lo_done, pair_of + 1)
                        mine = rows(n)
                        nc.vector.tensor_tensor(o_pair[mine, :], pv_bank[n][mine, :], o_part[mine, :],
                                                ALU.add).then_inc(o_sum_done, 1)
                    elif kind == "D":
                        mean_squares(it * TT + TT, n)
                    elif kind == "M":
                        if n == 0:
                            dve.wait_ge(flip_full, u0 + (places["T1"][0] + 1))
                        stage_qk(it * TT + TT, n)
                    elif kind == "L":
                        split_lo(j + 1, 0 if next_x else "qkv", 2 * n)

            def add_residual(b, c, tt):
                g = c * TT + tt
                _, n = OUT_COLS[c]
                dve.wait_ge(proj_done, out_job(b, c) * TT + (tt + 1))
                dve.wait_ge(res_loaded[g % NRES], b * (16 * NOUT * TT // NRES) + 16 * (g // NRES + 1))
                nc.vector.tensor_tensor(res[g % NRES][:, 0:n], proj_bank[tt % 2][:, 0:n],
                                        res[g % NRES][:, 0:n], ALU.add).then_inc(proj_drained, 1)

            dve.sem_inc(o_sum_done, CREDIT)
            for head in range(2):
                nc.vector.memset(f32(k_lo[head][rows(1 - head), :]), 0.0)
            for kt in range(0, KT, 2):
                split_lo(0, "qkv", kt)
            scale_x(0, 0)
            scale_x(0, 1)
            dve.wait_ge(const_loaded, 16 * 5)
            nc.vector.tensor_scalar(gq_col[:, :], gq_raw[:, :], DH ** -0.5, None, ALU.mult).then_inc(mod_step, 1)
            dve.wait_ge(mod_turned, 1)
            nc.vector.tensor_tensor(mod_t[:, :, :], pv_bank[0][:, 0:2 * KT * B].rearrange("p (c b) -> p c b", b=B),
                                    b_col[:, :].unsqueeze(2).to_broadcast([P, 2 * KT, B]),
                                    ALU.add).then_inc(mod_step, 1)
            dve.wait_ge(mod_step, 2)
            nc.vector.tensor_scalar(mod_t[:, 0:KT, :], mod_t[:, 0:KT, :], 1.0, None, ALU.add).then_inc(mod_step, 1)
            dve.wait_ge(mod_step, 3)
            by_batch = mod[:, :, :].rearrange("p b c -> p c b")
            nc.vector.tensor_tensor(by_batch[:, 0:KT, :], mod_t[:, 0:KT, :],
                                    g_col[:, :].unsqueeze(2).to_broadcast([P, KT, B]),
                                    ALU.mult).then_inc(mod_step, 1)
            nc.vector.tensor_copy(by_batch[:, KT:2 * KT, :], mod_t[:, KT:2 * KT, :]).then_inc(mod_step, 1)
            dve.wait_ge(mod_step, 5)
            nc.vector.tensor_copy(mod_now[:, :], mod[:, 0, :]).then_inc(mod_now_done, 1)
            dve.wait_ge(mod_now_done, 1)
            modulate(0, 0, 0, 0, first=True)
            scale_x(0, 2)
            modulate(0, 0, 2, 1, first=True)
            scale_x(0, 3)
            modulate(0, 0, 4, 2, first=True)
            modulate(0, 0, 6, 3, first=True)
            dve.wait_ge(wo_loaded, 16)
            dve.wait_ge(ident_ready, 1)
            for kt in range(KT):
                d = wo_raw[:, kt, kt * P:(kt + 1) * P]
                op = nc.vector.tensor_tensor(d, d, ident[:, :], ALU.add)
            op.then_inc(wo_ready, 1)
            for tt in range(TT):
                mean_squares(0, tt)
                stage_qk(0, tt)
            for kt in range(0, KT, 2):
                split_lo(1, "qkv", kt)

            with dve.Fori(0, B) as b:
                pair(b, 0, STEPS_FIRST, False)
                with dve.Fori(1, PAIRS - 2) as p:
                    pair(b, p, STEPS, False)
                pair(b, PAIRS - 2, STEPS_X, False)
                pair(b, PAIRS - 1, STEPS_LAST, True)
                for c in range(NOUT):
                    for tt in range(TT):
                        add_residual(b, c, tt)
                    for kt in range(0, KT, 2):
                        split_lo(out_job(b, c) + 1, next_kind(c), kt)

        @block.gpsimd
        def _(pool):
            def split_lo(j, kind, kt):
                src, n = w_source(kind, kt)
                pool.wait_ge(w_hi_done, j * KT + (kt + 1))
                nc.gpsimd.tensor_tensor(w_split[:, kt, 1, 0:n], src, f32(w_split[:, kt, 0, 0:n]),
                                        ALU.subtract).then_inc(w_lo_odd, 1)

            def rstd_x(n, r):
                pool.wait_ge(x_ms_done, n + (r + 1))
                nc.gpsimd.tensor_tensor(x_rstd[r % 2][:, :], x_ms_eps[r % 2][:, :], neg_half[:, 0:1],
                                        ALU.pow).then_inc(x_rstd_done, 1)

            def rstd_qk(q, tt):
                pool.wait_ge(qk_eps_done, q + (tt + 1))
                nc.gpsimd.tensor_tensor(qk_rstd[:, tt, :], qk_ms_eps[:, tt, :], neg_half[:, :],
                                        ALU.pow).then_inc(qk_rstd_done, 1)

            def xn_low(n, r):
                for half in range(2):
                    pool.wait_ge(xn_hi_done, n + (2 * r + half + 1))
                    cols = slice(4 * half, 4 * half + 4), slice(r * P, (r + 1) * P)
                    nc.gpsimd.tensor_tensor(xn_lo[:, cols[0], cols[1]],
                                            y_half[half][:, :].rearrange("p (k t) -> p k t", k=4),
                                            f32(xn_hi[:, cols[0], cols[1]]),
                                            ALU.subtract).then_inc(xn_lo_done, 1)

            def pair(b, p, steps, next_x):
                it, j = pair_no(b, p), job_no(b, p)
                for step in steps:
                    kind, n = step[0].upper(), int(step[1:])
                    if kind == "V":
                        pool.wait_ge(v_hi_done, it * 2 + (n + 1))
                        nc.gpsimd.tensor_tensor(v_split[n][:, :, rows(1 - n)], v_part(p, n),
                                                f32(v_split[n][:, :, rows(n)]), ALU.subtract).then_inc(v_lo_done, 1)
                    elif kind == "A":
                        rstd_x(b * TT + TT, n)
                    elif kind == "X":
                        xn_low(b * FLIP_X + FLIP_X, n)
                    elif kind == "Q":
                        left_over = step[0] == "q"
                        pool.wait_ge(o_hi_done, it + (0 if left_over else 1))
                        place = bass.ds(p - 1 if left_over else p, 1)
                        nc.gpsimd.tensor_tensor(o_lo[:, place, :], o_pair[:, :].unsqueeze(1), f32(o_hi[:, place, :]),
                                                ALU.subtract).then_inc(o_lo_done, 1)
                    elif kind == "D":
                        rstd_qk(it * TT + TT, n)
                    elif kind == "L":
                        split_lo(j + 1, 0 if next_x else "qkv", 2 * n + 1)

            pool.sem_inc(v_lo_done, CREDIT)
            pool.sem_inc(o_lo_done, 1)
            nc.gpsimd.memset(neg_half[:, :], -0.5)
            nc.gpsimd.memset(ident[:, :], 0.0).then_inc(ident_zero, 1)
            pool.wait_ge(ident_zero, 1)
            nc.gpsimd.affine_select(out=ident[:, :], in_=ident[:, :], compare_op=ALU.not_equal, fill=1.0, base=0,
                                    pattern=[[-1, P]], channel_multiplier=1).then_inc(ident_ready, 1)
            pool.wait_ge(ident_ready, 1)
            for kt in range(1, KT, 2):
                split_lo(0, "qkv", kt)
            rstd_x(0, 0)
            rstd_x(0, 1)
            xn_low(0, 0)
            rstd_x(0, 2)
            xn_low(0, 1)
            rstd_x(0, 3)
            xn_low(0, 2)
            xn_low(0, 3)
            for tt in range(TT):
                rstd_qk(0, tt)
            for kt in range(1, KT, 2):
                split_lo(1, "qkv", kt)

            with pool.Fori(0, B) as b:
                pair(b, 0, STEPS_FIRST, False)
                with pool.Fori(1, PAIRS - 2) as p:
                    pair(b, p, STEPS, False)
                pair(b, PAIRS - 2, STEPS_X, False)
                pair(b, PAIRS - 1, STEPS_LAST, True)
                for c in range(NOUT):
                    for kt in range(1, KT, 2):
                        split_lo(out_job(b, c) + 1, next_kind(c), kt)

        def load_res(sp, b, g):
            c, tt = divmod(g, TT)
            c0, n = OUT_COLS[c]
            sp.wait_ge(res_stored[g % NRES], b * (16 * NOUT * TT // NRES) + 16 * (g // NRES + 1))
            sp.dma_start(res[g % NRES][:, 0:n].unsqueeze(1),
                         x_rows[bass.ds(b, 1), tt, :, c0:c0 + n].rearrange("a p d -> p a d")
                         ).then_inc(res_loaded[g % NRES], 16)

        @block.sync
        def _(sp):
            def load_pair(pair_index, after=None):
                for half in range(2):
                    if after is not None:
                        sp.wait_ge(w_lo_even, after * (KT // 2) + 2 * (half + 1))
                        sp.wait_ge(w_lo_odd, after * (KT // 2) + 2 * (half + 1))
                    kts = slice(4 * half, 4 * half + 4)
                    sp.dma_start(w_raw[:, kts, :].unsqueeze(1),
                                 w_pair[bass.ds(pair_index, 1), :, kts, :].rearrange("a p k n -> p a k n")
                                 ).then_inc(raw_loaded[half], 16)

            def load_x(nb, r):
                sp.dma_start(x_tile[r % 2][:, :].unsqueeze(1),
                             x_rows[bass.ds(nb, 1), r, :, :].rearrange("a p d -> p a d")
                             ).then_inc(x_loaded[r % 2], 16)

            nc_const = [
                (cond_sb[:, :, :], cond_t),
                (b_col[:, :], b_emb),
                (g_col[:, :], g_norm),
                (gq_raw[0:P, :], g_q.rearrange("(p a) -> p a", a=1)),
                (gk_col[0:P, :], g_k.rearrange("(p a) -> p a", a=1)),
            ]
            for i in range(NRES):
                sp.sem_inc(res_stored[i], 16)
            for dst, src in nc_const:
                sp.dma_start(dst, src).then_inc(const_loaded, 16)
            emb_rows = w_emb.rearrange("(k p) (c n) -> k p c n", p=P, n=512)
            for kt in range(KT):
                if kt >= 2:
                    sp.wait_ge(emb_used, kt - 1)
                sp.dma_start(emb_tile[kt % 2][:, :, :], emb_rows[kt]).then_inc(emb_loaded[kt % 2], 16)
                if kt == 0:
                    load_x(0, 0)
                if kt == 1:
                    load_x(0, 1)
                    load_pair(0)
            load_pair(1, after=0)
            for r in range(2, TT):
                sp.wait_ge(xn_lo_done, 2 * (r - 2) + 2)
                load_x(0, r)
            sp.dma_start(wo_raw[:, :, :], w_out.rearrange("(k p) n -> p k n", p=P)).then_inc(wo_loaded, 16)
            load_pair(2, after=1)

            with sp.Fori(0, B) as b:
                for r in range(TT):
                    if r == 2:
                        with sp.Fori(0, PAIRS - 2) as p:
                            load_pair((p + 3) % PAIRS, after=job_no(b, p) + 1)
                    sp.wait_ge(xn_lo_done, b * FLIP_X + (FLIP_X + 2 * (r - 2) + 2))
                    load_x((b + 1) % B, r)
                load_pair((PAIRS + 1) % PAIRS, after=job_no(b, PAIRS - 2) + 1)
                for c, (c0, n) in enumerate(OUT_COLS):
                    for tt in range(TT):
                        g = c * TT + tt
                        if g == 0:
                            for early in range(NRES - 1):
                                load_res(sp, b, early)
                        if g + NRES - 1 < NOUT * TT:
                            load_res(sp, b, g + NRES - 1)
                        sp.wait_ge(proj_drained, out_job(b, c) * TT + (tt + 1))
                        sp.dma_start(out_rows[bass.ds(b, 1), tt, :, c0:c0 + n].rearrange("a p d -> p a d"),
                                     res[g % NRES][:, 0:n].unsqueeze(1)).then_inc(res_stored[g % NRES], 16)
                load_pair(2, after=out_job(b, NOUT - 1) + 1)
            for i in range(NRES):
                sp.wait_ge(res_stored[i], B * 16 * NOUT * TT // NRES + 16)
            for half in range(2):
                sp.wait_ge(raw_loaded[half], 16 * (B * PAIRS + 3))
            for i in range(2):
                sp.wait_ge(x_loaded[i], 32 * (B + 1))

def kernel(x, cond_2048, L0_cond_W_emb, L0_cond_b_emb, L0_cond_g_norm, L0_cond_W_qkv, L0_cond_g_q, L0_cond_g_k,
           L0_cond_W_out):
    import numpy as np
    import concourse.bacc as bacc
    from concourse.bass_utils import run_bass_kernel_spmd

    w = np.asarray(L0_cond_W_qkv).reshape(D, 3, PAIRS, P).transpose(2, 0, 1, 3).reshape(PAIRS, D, QKV)
    data = {
        "x": np.ascontiguousarray(x),
        "cond_t": np.ascontiguousarray(np.asarray(cond_2048).T.reshape(KT, P, B).transpose(1, 0, 2)),
        "w_emb": np.ascontiguousarray(L0_cond_W_emb),
        "b_emb": np.ascontiguousarray(np.asarray(L0_cond_b_emb).reshape(2 * KT, P).T),
        "g_norm": np.ascontiguousarray(np.asarray(L0_cond_g_norm).reshape(KT, P).T),
        "w_qkv": np.ascontiguousarray(w),
        "g_q": np.concatenate([np.asarray(L0_cond_g_q)] * 2),
        "g_k": np.concatenate([np.asarray(L0_cond_g_k)] * 2),
        "w_out": np.ascontiguousarray(L0_cond_W_out),
    }
    nc = bacc.Bacc("TRN2", target_bir_lowering=False, num_devices=1)
    args = [nc.dram_tensor(f"in_{k}", a.shape, mybir.dt.from_np(a.dtype), kind="ExternalInput").ap()
            for k, a in data.items()]
    out = nc.dram_tensor("out_0", (B, T, D), F32, kind="ExternalOutput").ap()
    cond_attention(nc, *args, out)
    r = run_bass_kernel_spmd(nc, [{f"in_{k}": a for k, a in data.items()}], core_ids=[0])
    return r.results[0]["out_0"]
```

```python
from contextlib import ExitStack

import concourse.bass as bass
from concourse import mybir

F32 = mybir.dt.float32
F32R = mybir.dt.float32r
BF16 = mybir.dt.bfloat16
ALU = mybir.AluOpType
ACT = mybir.ActivationFunctionType
AX = mybir.AxisListType

P = 128
B, T, D = 8, 512, 1024
H, DH = 16, 64
PAIRS = H // 2
KT = D // P
TT = T // P
QKV = 3 * P
EPS = 1e-6
OUT_COLS = [(0, 384), (384, 384), (768, 256)]
NOUT = len(OUT_COLS)


JOBS = PAIRS + NOUT
FLIP_X = 2 * TT
FLIP_PAIR = 2 + 2 * TT
CREDIT = 2

PAIR = {
    "TensorE": """
        C0 f2 w0 w1 f3 C1 T0 w2 T1 C2 C3 C4 w3 S0 S1 C5 S2 C6 S3 C7 S4 C8 S5 F0 C9 F1 C10 S6 F2 C11 W0 F3 W1 C12
        S7 W2 W3 C13 C14 F4 F5 C15""".split(),
    "ScalarE": """
        V0 f2 f3 T0 T1 D0 o1 q0 S0 V1 S1 S2 S3 D1 F0 S4 F1 S5 S6 F2 D2 F3 L0 S7 O0 L1 L2 F4 F5 D3 L3""".split(),
    "VectorE": """
        f2 f3 T0 T1 o1 D0 S0 S1 N0 S2 N1 S3 M0 N2 N3 S4 D1 F0 N4 S5 F1 S6 M1 N5 F2 D2 F3 S7 N6 L0 N7 M2 O0 L1 L2
        F4 F5 D3 L3 M3""".split(),
    "GpSimd": """
        q0 V0 D0 D1 D2 V1 L0 L1 D3 L2 L3""".split(),
}
FIRST_PAIR = {
    "TensorE": """
        C0 T0 T1 C1 C4 C2 C3 S0 S1 C5 C6 S2 C7 S3 C8 S4 F0 S5 C9 F1 F2 W0 C10 S6 F3 C11 W1 W2 C12 S7 W3 C13 C14
        F4 F5 C15""".split(),
    "ScalarE": """
        V0 T0 T1 D0 V1 S0 S1 S2 D1 S3 F0 S4 F1 F2 S5 S6 D2 F3 L0 S7 O0 L1 L2 F4 F5 D3 L3""".split(),
    "VectorE": """
        T0 T1 D0 S0 M0 N0 S1 S2 N1 D1 S3 N2 N3 S4 F0 S5 M1 F1 F2 S6 N4 D2 F3 N5 S7 N6 L0 N7 M2 O0 L1 L2 F4 F5 D3
        L3 M3""".split(),
    "GpSimd": """
        D0 V0 D1 D2 L0 L1 L2 V1 D3 L3""".split(),
}
TURNS_X_PAIR = {
    "TensorE": """
        C0 f2 w0 C1 w1 T0 w2 T1 f3 C2 C4 C3 w3 S0 C5 X0 S1 S2 C6 C7 C8 S3 S4 X1 F0 C9 S5 F1 C10 F2 W0 S6 W1 F3 S7
        C11 W2 C12 W3 X2 C13 C14 F4 F5 C15""".split(),
    "ScalarE": """
        f2 A0 T0 V0 A1 T1 f3 D0 o1 S0 q0 S1 V1 X0 S2 D1 S3 S4 X1 F0 S5 F1 A2 F2 S6 F3 D2 L0 S7 A3 L1 X2 F4 F5 L2
        D3 L3 O0""".split(),
    "VectorE": """
        f2 B0 A0 T0 T1 f3 D0 S0 o1 S1 X0 M0 N0 A1 N1 S2 N2 D1 S3 N3 S4 X1 M1 S5 F0 N4 F1 F2 N5 S6 A2 F3 S7 D2 N6
        N7 X2 L0 A3 M2 F4 L1 L2 F5 D3 O0 L3 M3""".split(),
    "GpSimd": """
        A0 V0 D0 A1 X0 D1 V1 X1 A2 q0 D2 L0 A3 X2 L1 D3 L2 L3""".split(),
}
LAST_PAIR = {
    "TensorE": """
        C0 f2 w0 f3 C1 w1 T0 w2 T1 C2 w3 C3 C4 S0 S1 C5 S2 X3 C6 C7 S3 S4 C8 S5 F0 C9 S6 C10 F1 W0 F2 C11 F3 W1
        C12 S7 W2 W3 C13 C14 F4 F5 C15""".split(),
    "ScalarE": """
        V0 f2 f3 T0 T1 D0 o1 S0 q0 S1 S2 X3 S3 V1 D1 S4 F0 F1 S5 S6 F2 D2 F3 L0 S7 O0 L1 L2 F4 F5 D3 L3""".split(),
    "VectorE": """
        f2 f3 T0 T1 o1 S0 D0 S1 S2 X3 N0 M0 N1 S3 N2 N3 S4 D1 F0 M1 S5 S6 F1 N4 N5 F2 D2 F3 S7 N6 M2 L0 N7 O0 L1
        L2 F4 F5 D3 M3 L3""".split(),
    "GpSimd": """
        V0 q0 D0 X3 D1 D2 V1 L0 L1 L2 D3 L3""".split(),
}
OUT_PAIR = {
    "TensorE": """
        P0 w0 P1 f2 w1 f3 P4 T0 P5 T1 P2 P6 w2 w3 S0 S1 P3 P7 P8 P9 P10 P11 P12 P13 S2 S3 P14 P15 P16 P17 P18 P20
        P19 P21 P24 P22 S4 P23 P25 S5 P28 P29 P26 F0 P27 P30 F1 P32 W0 P31 W1 P33 P34 S6 P36 P37 P35 F2 F3 S7 P38
        P39 P40 W2 P41 P44 W3 P45 P42 P46 P43 F4 F5 C0 P47 C1 C4 C2 C3 C5 C6 C7 C8 C9 C10 C11 C12 C13 C14 C15""".split(),
    "ScalarE": """
        V0 f2 f3 T0 T1 o1 q0 S0 S1 K0 K1 V1 S2 K2 K3 S3 K4 K5 S4 F0 F1 K6 S5 K7 F2 F3 S6 S7 K8 K9 O0 F4 K10 K11
        F5 D0 D1 D2 L0 L1 L2 D3 L3""".split(),
    "VectorE": """
        f2 f3 T0 o1 T1 S0 R0 S1 R1 R2 K0 K1 S2 K2 K3 R3 N0 N1 R4 S3 N2 N3 S4 R5 K4 K5 S5 F0 R6 F1 K6 K7 R7 S6 R8
        N4 N5 F2 F3 R9 S7 K8 N6 N7 K9 O0 R10 K10 F4 R11 F5 K11 D0 M0 D1 M1 D2 M2 L0 D3 L1 L2 L3 M3""".split(),
    "GpSimd": """
        V0 q0 V1 K0 K1 K2 K3 K4 K5 K6 K7 K8 K9 K10 K11 D0 D1 D2 L0 L1 L2 D3 L3""".split(),
}
FINAL_PAIR = {
    "TensorE": """
        f2 w0 w1 f3 T0 w2 T1 w3 S0 S1 S2 S3 S4 S5 F0 F1 P0 F2 W0 F3 W1 S6 S7 W2 W3 P1 P2 F4 F5 P4 P5 P6 F6 W4 F7
        W5 W6 W7 P3 P7 P8 P9 P10 P11 P12 P13 P14 P15 P16 P17 P18 P19 P20 P24 P21 P22 P23 P25 P26 P27 P28 P29 P30
        P31 P32 P33 P34 P36 P35 P37 P38 P39 P40 P41 P44 P45 P42 P43 P46 P47""".split(),
    "ScalarE": """
        V0 f2 f3 T0 T1 o1 S0 q0 S1 S2 S3 S4 F0 F1 F2 S5 F3 V1 O0 S6 S7 F4 F5 F6 F7 O1 Q0 K0 K1 K2 K3 K4 K5 K6 K7""".split(),
    "VectorE": """
        f2 f3 T0 T1 o1 S0 S1 N0 S2 N1 S3 N2 N3 S4 F0 S5 N4 F1 F2 N5 F3 S6 S7 N6 N7 F4 O0 F5 F6 F7 O1 R0 R1 K0 K1
        R2 K2 K3 R3 R4 R5 R6 K4 K5 K6 R7 K7 R8 R9 R10 R11""".split(),
    "GpSimd": """
        V0 q0 V1 Q0 K0 K1 K2 K3 K4 K5 K6 K7""".split(),
}
LEFT = sum(step[0] == "f" for step in PAIR["TensorE"])
EARLY_X = sum(step[0] == "X" for step in TURNS_X_PAIR["TensorE"])


def flip_places(order):
    places, u, v = {}, 0, 0
    for step in order["TensorE"]:
        if step[0] in "TFfX":
            places[step] = u, v
            u, v = u + (2 if step[0] == "X" else 1), v + (step[0] != "X")
    return places


def cond_attention(nc, x, cond_t, w_emb, b_emb, g_norm, w_qkv, g_q, g_k, w_out, out):
    x_rows = x.rearrange("b (t p) d -> b t p d", p=P)
    out_rows = out.rearrange("b (t p) d -> b t p d", p=P)
    w_pair = w_qkv.rearrange("a (k p) n -> a p k n", p=P)

    with ExitStack() as ctx:
        def sb(name, shape, dt=F32):
            return ctx.enter_context(nc.sbuf_tensor(name, shape, dt))

        def sem(name):
            return ctx.enter_context(nc.semaphore(name))

        def bank(name):
            return ctx.enter_context(nc.psum_tensor(name, [P, 512], F32))

        proj_bank = [bank(f"proj_bank{i}") for i in range(2)]
        score_bank = [bank(f"score_bank{i}") for i in range(2)]
        flip_bank = [bank(f"flip_bank{i}") for i in range(2)]
        pv_bank = [bank(f"pv_bank{i}") for i in range(2)]

        w_raw = sb("w_raw", [P, KT, QKV])
        w_split = sb("w_split", [P, KT, 2, QKV], F32R)
        wo_raw = sb("wo_raw", [P, KT, D])
        xn_hi = sb("xn_hi", [P, KT, T], F32R)
        xn_lo = sb("xn_lo", [P, KT, T], F32R)
        o_hi = sb("o_hi", [P, PAIRS, T], F32R)
        o_lo = sb("o_lo", [P, PAIRS, T], F32R)
        qk_stage = sb("qk_stage", [P, TT, 2 * P])
        v_stage = sb("v_stage", [P, 2, TT, P])
        q_split = [sb(f"q_split{h}", [P, T], F32R) for h in range(2)]
        k_hi = [sb(f"k_hi{h}", [P, T], F32R) for h in range(2)]
        k_lo = [sb(f"k_lo{h}", [P, T], F32R) for h in range(2)]
        v_split = [sb(f"v_split{h}", [P, TT, P], F32R) for h in range(2)]
        probs = [sb(f"probs{h}", [P, TT, T]) for h in range(2)]
        pt_hi = [sb(f"pt_hi{i}", [P, T], F32R) for i in range(2)]
        pt_lo = [sb(f"pt_lo{i}", [P, T], F32R) for i in range(2)]
        x_tile = [sb(f"x_tile{i}", [P, D]) for i in range(2)]
        y_half = [sb(f"y_half{i}", [P, 512]) for i in range(2)]
        square_out = sb("square_out", [P, D], BF16)
        sq = [sb(f"sq{i}", [P, 2 * P]) for i in range(2)]
        o_part = sb("o_part", [P, T])
        o_pair = sb("o_pair", [P, T])
        NRES = 3
        res = [sb(f"res{i}", [P, 384]) for i in range(NRES)]
        ident = sb("ident", [P, P])
        neg_half = sb("neg_half", [P, 4])
        eps_col = sb("eps_col", [P, 4])
        cond_sb = sb("cond_sb", [P, KT, B])
        b_col = sb("b_col", [P, 2 * KT])
        g_col = sb("g_col", [P, KT])
        gq_raw = sb("gq_raw", [P, 1])
        gq_col = sb("gq_col", [P, 1])
        gk_col = sb("gk_col", [P, 1])
        mod_t = sb("mod_t", [P, 2 * KT, B])
        mod = sb("mod", [P, B, 2 * KT])
        mod_now = sb("mod_now", [P, 2 * KT])
        x_ms = [sb(f"x_ms{i}", [P, 1]) for i in range(TT)]
        x_ms_eps = [sb(f"x_ms_eps{i}", [P, 1]) for i in range(TT)]
        x_rstd = [sb(f"x_rstd{i}", [P, 1]) for i in range(TT)]
        qk_ms = sb("qk_ms", [P, TT, 4])
        qk_ms_eps = sb("qk_ms_eps", [P, TT, 4])
        qk_rstd = sb("qk_rstd", [P, TT, 4])
        neg_max = sb("neg_max", [P, 8])
        row_sum = sb("row_sum", [P, 8])
        row_inv = sb("row_inv", [P, 8])
        emb_tile = [probs[0][:, :, :], probs[1][:, :, :]] + [
            wo_raw[:, 2 * i:2 * i + 2, :].rearrange("p a (c n) -> p (a c) n", n=512) for i in range(KT // 2)]
        NEMB = len(emb_tile)

        def emb_slot(kt):
            return (kt, 1) if kt < NEMB else (2 * (kt - NEMB), 2)

        first_x = [x_tile[0][:, :], x_tile[1][:, :]] + [
            probs[1][:, 2 * i:2 * i + 2, :].rearrange("p a n -> p (a n)") for i in range(2)]
        mod_rows = probs[0][0:B, :, :]

        const_loaded = sem("const_loaded")
        emb_loaded = [sem(f"emb_loaded{i}") for i in range(NEMB)]
        first_x_loaded = [sem(f"first_x_loaded{i}") for i in range(2)]
        emb_used = sem("emb_used")
        ident_zero = sem("ident_zero")
        ident_ready = sem("ident_ready")
        mod_rows_ready = sem("mod_rows_ready")
        mod_turned = sem("mod_turned")
        mod_step = sem("mod_step")
        wo_loaded = sem("wo_loaded")
        wo_ready = sem("wo_ready")
        raw_loaded = [sem(f"raw_loaded{i}") for i in range(2)]
        w_hi_done = sem("w_hi_done")
        w_lo_even = sem("w_lo_even")
        w_lo_odd = sem("w_lo_odd")
        w_used = sem("w_used")
        x_loaded = [sem(f"x_loaded{i}") for i in range(2)]
        x_squared = sem("x_squared")
        x_eps_done = sem("x_eps_done")
        x_rstd_done = sem("x_rstd_done")
        x_scaled = sem("x_scaled")
        mod_now_done = sem("mod_now_done")
        xn_hi_done = sem("xn_hi_done")
        xn_lo_done = sem("xn_lo_done")
        proj_done = sem("proj_done")
        proj_drained = sem("proj_drained")
        v_staged = sem("v_staged")
        v_hi_done = sem("v_hi_done")
        v_lo_done = sem("v_lo_done")
        sq_done = sem("sq_done")
        qk_ms_done = sem("qk_ms_done")
        qk_eps_done = sem("qk_eps_done")
        qk_rstd_done = sem("qk_rstd_done")
        flip_full = sem("flip_full")
        flip_hi = sem("flip_hi")
        flip_free = sem("flip_free")
        score_full = sem("score_full")
        max_done = sem("max_done")
        exp_done = sem("exp_done")
        inv_done = sem("inv_done")
        probs_ready = sem("probs_ready")
        pv_used = sem("pv_used")
        o_part_done = sem("o_part_done")
        o_sum_done = sem("o_sum_done")
        o_hi_done = sem("o_hi_done")
        o_lo_done = sem("o_lo_done")
        res_loaded = [sem(f"res_loaded{i}") for i in range(NRES)]
        res_stored = [sem(f"res_stored{i}") for i in range(NRES)]

        def pair_no(b, p):
            return b * PAIRS + p

        def first(b, p):
            return isinstance(b, int) and isinstance(p, int) and b == 0 and p == 0

        def flip_hi_no(b, p):
            return 0 if first(b, p) else pair_no(b, p) * FLIP_PAIR - LEFT

        def flip_no(b, p, next_x=False):
            return flip_hi_no(b, p) + b * FLIP_X + (FLIP_X + 2 * EARLY_X if next_x else FLIP_X)

        def job_no(b, p):
            return b * JOBS + p + 1

        def own_job_end(b, p):
            return job_no(b, p) if first(b, p) or not (isinstance(p, int) and p == 0) else job_no(b, p) - NOUT

        def out_job(b):
            return b * JOBS + (PAIRS if isinstance(b, int) and b == B - 1 else PAIRS + 1)

        def f32(ap):
            return ap.bitcast(F32)

        def rows(head):
            return slice(head * DH, head * DH + DH)

        def w_source(job_kind, kt):
            if job_kind == "qkv":
                return w_raw[:, kt, :], QKV
            c0, n = OUT_COLS[job_kind]
            return wo_raw[:, kt, c0:c0 + n], n

        def o_place(p, step):
            return p if step[0] == "Q" else PAIRS - 1 if isinstance(p, int) and p == 0 else p - 1

        def kind_after(chunk):
            return chunk + 1 if chunk + 1 < NOUT else "qkv"

        def out_piece(n):
            return n // (4 * TT), n // 4 % TT, n % 4

        def v_part(p, head):
            return v_stage[:, bass.ds(p % 2, 1), :, rows(head)].rearrange("p a t d -> p (a t) d")

        def batches(engine, pair):
            pair(0, 0, FIRST_PAIR)
            with engine.Fori(0, B - 1) as b:
                with engine.Fori(1, PAIRS - 2) as p:
                    pair(b, p, PAIR)
                pair(b, PAIRS - 2, TURNS_X_PAIR)
                pair(b, PAIRS - 1, LAST_PAIR, next_x=True, next_kind=0)
                pair(b + 1, 0, OUT_PAIR, out_b=b)
            with engine.Fori(1, PAIRS - 2) as p:
                pair(B - 1, p, PAIR)
            pair(B - 1, PAIRS - 2, PAIR, next_kind=0)
            pair(B - 1, PAIRS - 1, FINAL_PAIR, out_b=B - 1)

        block = ctx.enter_context(nc.Block())

        @block.tensor
        def _(pe):
            def product(j, tt, piece, n, act_hi, act_lo, wait_bank=True):
                dst = proj_bank[tt % 2][:, 0:n]
                if piece == 0 and wait_bank:
                    pe.wait_ge(proj_drained, j * TT + (tt - 1))
                for kt in (2 * piece, 2 * piece + 1):
                    if tt == 0:
                        pe.wait_ge(w_lo_odd if kt % 2 else w_lo_even, j * (KT // 2) + (kt // 2 + 1))
                    a_hi = act_hi[:, kt, tt * P:(tt + 1) * P]
                    a_lo = act_lo[:, kt, tt * P:(tt + 1) * P]
                    w_hi, w_lo = w_split[:, kt, 0, 0:n], w_split[:, kt, 1, 0:n]
                    nc.tensor.matmul(dst, a_hi, w_hi, start=(kt == 0), stop=False)
                    nc.tensor.matmul(dst, a_hi, w_lo, start=False, stop=False)
                    mm = nc.tensor.matmul(dst, a_lo, w_hi, start=False, stop=(kt == KT - 1))
                    if tt == TT - 1 and kt < KT - 1:
                        mm.then_inc(w_used, 1)
                    if kt == KT - 1:
                        mm.then_inc(proj_done, 1)

            def turn_x(u0, u, n, r, tiles, wait_bank=True):
                for half in range(2):
                    if wait_bank:
                        pe.wait_ge(flip_free, u0 + (u + half - 1))
                    if half == 0:
                        pe.wait_ge(x_scaled, n + (r + 1))
                    for i in range(4):
                        kt = 4 * half + i
                        mm = nc.tensor.transpose(flip_bank[(u + half) % 2][:, i * P:(i + 1) * P],
                                                 tiles[r % len(tiles)][:, kt * P:(kt + 1) * P], ident[:, :])
                    mm.then_inc(flip_full, 1)

            def pair(b, p, order, next_x=False, next_kind="qkv", out_b=None):
                it, u0, j, places = pair_no(b, p), flip_no(b, p, next_x), job_no(b, p), flip_places(order)
                for step in order["TensorE"]:
                    kind, n, pair_of = step[0].upper(), int(step[1:]), it
                    if step[0] in "fw":
                        n, pair_of = n + 4, it - 1
                    if step[0] in "oq":
                        pair_of = it - 1
                    h, i = n // 4, n % 4
                    u, u_hi = places.get(step, (0, 0))
                    if kind == "T":
                        pe.wait_ge(flip_free, u0 + (u - 1))
                        if n == 0:
                            pe.wait_ge(proj_drained, own_job_end(b, p) * TT)
                        for tt in range(TT):
                            mm = nc.tensor.transpose(flip_bank[u % 2][:, tt * P:(tt + 1) * P],
                                                     qk_stage[:, tt, n * P:(n + 1) * P], ident[:, :])
                        mm.then_inc(flip_full, 1)
                    elif kind == "X":
                        turn_x(u0, u, b * TT + TT, n, x_tile)
                    elif kind == "C":
                        if next_x and i == 0:
                            pe.wait_ge(xn_lo_done, b * FLIP_X + (FLIP_X + 2 * h + 2))
                        product(j, h, i, QKV, xn_hi, xn_lo)
                    elif kind == "P":
                        c, tt, piece = out_piece(n)
                        if c == 0 and tt < 2 and piece in (0, 3):
                            pe.wait_ge(o_lo_done, out_b * PAIRS + (PAIRS + (1 if piece == 3 else 0)))
                        product(out_job(out_b) + c, tt, piece, OUT_COLS[c][1], o_hi, o_lo)
                    elif kind == "S":
                        pe.wait_ge(exp_done, it * 8 + (n - 2 + 1 + CREDIT))
                        if i == 0:
                            pe.wait_ge(flip_free, u0 + (places["T1"][0] + 1))
                        q_t = q_split[h][:, i * P:(i + 1) * P]
                        nc.tensor.matmul(score_bank[n % 2][:, :], q_t, k_hi[h][:, :], start=True, stop=False)
                        nc.tensor.matmul(score_bank[n % 2][:, :], q_t, k_lo[h][:, :], start=False,
                                         stop=True).then_inc(score_full, 1)
                    elif kind == "F":
                        pe.wait_ge(flip_free, u0 + (u - 1))
                        if i == 0:
                            pe.wait_ge(probs_ready, pair_of * 8 + (4 * h + 4))
                        for qt in range(TT):
                            mm = nc.tensor.transpose(flip_bank[u % 2][:, qt * P:(qt + 1) * P],
                                                     probs[h][:, qt, i * P:(i + 1) * P], ident[:, :])
                        mm.then_inc(flip_full, 1)
                    elif kind == "W":
                        if i == 0:
                            pe.wait_ge(o_sum_done, pair_of * 2 + (h - 1 + CREDIT))
                            pe.wait_ge(v_lo_done, pair_of * 2 + (h + 1 + CREDIT))
                        turned = places.get(("f" if step[0] == "w" else "F") + step[1:], (-1, -1))[0]
                        pe.wait_ge(flip_free, u0 + (turned + 1))
                        v_t = v_split[h][:, i, :]
                        nc.tensor.matmul(pv_bank[h][:, :], v_t, pt_hi[n % 2][:, :], start=(i == 0), stop=False)
                        nc.tensor.matmul(pv_bank[h][:, :], v_t, pt_lo[n % 2][:, :], start=False,
                                         stop=(i == TT - 1)).then_inc(pv_used, 1)

            pe.sem_inc(pv_used, CREDIT)
            pe.wait_ge(const_loaded, 16 * 5)
            emb_bank = [proj_bank[0], proj_bank[1], score_bank[0], score_bank[1]]
            for kt in range(KT):
                slot, uses = emb_slot(kt)
                pe.wait_ge(emb_loaded[slot], 16 * uses)
                for c in range(4):
                    mm = nc.tensor.matmul(emb_bank[c][0:B, :], cond_sb[:, kt, :], emb_tile[slot][:, c, :],
                                          start=(kt == 0), stop=(kt == KT - 1))
                mm.then_inc(emb_used, 1)
            pe.wait_ge(ident_ready, 1)
            pe.wait_ge(mod_rows_ready, 1)
            for c in range(2 * KT):
                mm = nc.tensor.transpose(pv_bank[0][:, c * B:(c + 1) * B],
                                         mod_rows[:, c // 4, (c % 4) * P:(c % 4 + 1) * P], ident[0:B, 0:B])
            mm.then_inc(mod_turned, 1)
            for r in range(TT + 1):
                if r < TT:
                    turn_x(0, 2 * r, 0, r, first_x, wait_bank=r > 0)
                if r > 0:
                    pe.wait_ge(xn_lo_done, 2 * (r - 1) + 2)
                    for piece in range(4):
                        product(0, r - 1, piece, QKV, xn_hi, xn_lo, wait_bank=r > 2)

            batches(pe, pair)

        @block.scalar
        def _(act):
            def split_hi(j, kind, kt, wait_used=True):
                src, n = w_source(kind, kt)
                if wait_used:
                    if kt < KT - 1:
                        act.wait_ge(w_used, j * (KT - 1) + (kt + 1 - (KT - 1)))
                    else:
                        act.wait_ge(proj_done, j * TT)
                nc.scalar.copy(w_split[:, kt, 0, 0:n], src).then_inc(w_hi_done, 1)

            def square_x(n, r, first=False):
                if first:
                    act.wait_ge(x_loaded[r] if r < 2 else first_x_loaded[r - 2], 16)
                else:
                    act.wait_ge(x_loaded[r % 2], n * (2 * 16) + 16 * (r // 2))
                if not first or r > 0:
                    act.wait_ge(x_squared, n * TT + r)
                nc.scalar.activation(square_out[:, :], first_x[r] if first else x_tile[r % 2][:, :], ACT.Square, scale=D ** -0.5,
                                     accum_out=x_ms[r][:, :]).then_inc(x_squared, 1)

            def modulate(n, u0, u, r, first=False):
                act.wait_ge(flip_full, u0 + (u + 2))
                if not first or r > 0:
                    act.wait_ge(xn_lo_done, n * 2 + 2 * r)
                for i in range(4):
                    kt = KT // 2 + i
                    op = nc.scalar.activation(y_half[1][:, i * P:(i + 1) * P],
                                              flip_bank[(u + 1) % 2][:, i * P:(i + 1) * P], ACT.Identity,
                                              scale=mod_now[:, kt:kt + 1], bias=mod_now[:, KT + kt:KT + kt + 1])
                op.then_inc(flip_free, 1)

            def xn_high(n, u0, u, r, first=False):
                for half in range(2):
                    if half == 1:
                        modulate(n, u0, u, r, first)
                    act.wait_ge(flip_free, u0 + (u + half + 1))
                    nc.scalar.copy(xn_hi[:, 4 * half:4 * half + 4, r * P:(r + 1) * P],
                                   y_half[half][:, :].rearrange("p (k t) -> p k t", k=4)).then_inc(xn_hi_done, 1)

            def stage_v_square_qk(j, tt, stage):
                act.wait_ge(proj_done, j * TT + (tt + 1))
                nc.scalar.copy(v_stage[:, stage, tt, :], proj_bank[tt % 2][:, 2 * P:3 * P].unsqueeze(1)).then_inc(v_staged, 1)
                nc.scalar.activation(sq[tt % 2][:, :], proj_bank[tt % 2][:, 0:2 * P], ACT.Square,
                                     scale=DH ** -0.5).then_inc(sq_done, 1)

            def pair(b, p, order, next_x=False, next_kind="qkv", out_b=None):
                it, u0, j, places = pair_no(b, p), flip_no(b, p, next_x), job_no(b, p), flip_places(order)
                for step in order["ScalarE"]:
                    kind, n, pair_of = step[0].upper(), int(step[1:]), it
                    if step[0] in "fw":
                        n, pair_of = n + 4, it - 1
                    if step[0] in "oq":
                        pair_of = it - 1
                    h, i = n // 4, n % 4
                    u, u_hi = places.get(step, (0, 0))
                    if kind == "V":
                        act.wait_ge(v_staged, it * TT + TT)
                        act.wait_ge(pv_used, it * 8 + CREDIT if n == 1 or first(b, p) else it * 8 - 4 + CREDIT)
                        nc.scalar.copy(v_split[n][:, :, rows(n)], v_part(p, n)).then_inc(v_hi_done, 1)
                    elif kind == "T":
                        act.wait_ge(flip_full, u0 + (u + 1))
                        for head in range(2):
                            mine, other = rows(head), rows(1 - head)
                            if n == 0:
                                op = nc.scalar.activation(q_split[head][mine, :], flip_bank[u % 2][mine, :], ACT.Copy,
                                                          scale=gq_col[mine, :])
                            else:
                                for to in (mine, other):
                                    op = nc.scalar.activation(k_hi[head][to, :], flip_bank[u % 2][mine, :], ACT.Copy,
                                                              scale=gk_col[mine, :])
                        op.then_inc(flip_hi, 1)
                    elif kind == "A":
                        square_x(b + 1, n)
                    elif kind == "X":
                        act.wait_ge(proj_done, job_no(b, PAIRS - 2) * TT + (n + 1))
                        xn_high(b * TT + TT, u0, u, n)
                    elif kind == "S":
                        act.wait_ge(max_done, it * 8 + (n + 1))
                        if i == 0:
                            act.wait_ge(flip_full, u0 + (places["f3"][0] + 1 if h and "f3" in places else 0))
                        nc.scalar.activation(probs[h][:, i, :], score_bank[n % 2][:, :], ACT.Exp,
                                             bias=neg_max[:, n:n + 1],
                                             accum_out=row_sum[:, n:n + 1]).then_inc(exp_done, 1)
                    elif kind == "F":
                        act.wait_ge(flip_full, u0 + (u + 1))
                        act.wait_ge(pv_used, pair_of * 8 + (n - 1 + CREDIT))
                        nc.scalar.copy(pt_hi[n % 2][:, :], flip_bank[u % 2][:, :]).then_inc(flip_hi, 1)
                    elif kind == "O":
                        act.wait_ge(pv_used, pair_of * 8 + (4 * n + 4 + CREDIT))
                        act.wait_ge(o_sum_done, pair_of * 2 + (n - 1 + CREDIT))
                        mine, other = rows(n), rows(1 - n)
                        nc.scalar.copy(o_part[mine, :], pv_bank[n][other, :]).then_inc(o_part_done, 1)
                    elif kind == "Q":
                        act.wait_ge(o_sum_done, pair_of * 2 + (2 + CREDIT))
                        place = bass.ds(o_place(p, step), 1)
                        nc.scalar.copy(o_hi[:, place, :], o_pair[:, :].unsqueeze(1)).then_inc(o_hi_done, 1)
                    elif kind == "D":
                        if n == 0:
                            act.wait_ge(v_lo_done, it * 2 + CREDIT)
                        act.wait_ge(qk_ms_done, it * TT + (TT + n - 1))
                        stage_v_square_qk(j, n, bass.ds((p + 1) % 2, 1))
                    elif kind == "L":
                        if n % 2 == 0 and next_kind == "qkv":
                            act.wait_ge(raw_loaded[n // 2], it * 16 + 16 * 3)
                        if n == 0 and next_kind == 0:
                            act.wait_ge(wo_ready, 1)
                        for kt in (2 * n, 2 * n + 1):
                            split_hi(j + 1, next_kind, kt)
                    elif kind == "K":
                        if h == NOUT - 1 and i % 2 == 0:
                            act.wait_ge(raw_loaded[i // 2], out_b * (PAIRS * 16) + 16 * (PAIRS + 2))
                        for kt in (2 * i, 2 * i + 1):
                            split_hi(out_job(out_b) + h + 1, kind_after(h), kt)

            def split_second(kts):
                for kt in kts:
                    act.wait_ge(raw_loaded[kt // 4], 32)
                    split_hi(1, "qkv", kt)

            act.sem_inc(exp_done, CREDIT)
            for kt in range(KT):
                act.wait_ge(raw_loaded[kt // 4], 16)
                split_hi(0, "qkv", kt, wait_used=False)
            for r in range(TT):
                square_x(0, r, first=True)
            emb_bank = [proj_bank[0], proj_bank[1], score_bank[0], score_bank[1]]
            act.wait_ge(emb_used, KT)
            for c in range(4):
                cp = nc.scalar.copy(mod_rows[:, c, :], emb_bank[c][0:B, :])
            cp.then_inc(mod_rows_ready, 1)
            for r in range(TT + 1):
                if r < TT:
                    xn_high(0, 0, 2 * r, r, first=True)
                else:
                    split_second(range(0, KT - 2))
                if r > 0:
                    if r > 2:
                        act.wait_ge(qk_ms_done, r - 2)
                    stage_v_square_qk(0, r - 1, slice(0, 1))
            split_second(range(KT - 2, KT))

            batches(act, pair)

        @block.vector
        def _(dve):
            def split_lo(j, kind, kt):
                src, n = w_source(kind, kt)
                dve.wait_ge(w_hi_done, j * KT + (kt + 1))
                nc.vector.tensor_tensor(w_split[:, kt, 1, 0:n], src, f32(w_split[:, kt, 0, 0:n]),
                                        ALU.subtract).then_inc(w_lo_even, 1)

            def scale_x(n, r, tiles):
                dve.wait_ge(x_rstd_done, n + (r + 1))
                nc.vector.tensor_scalar(tiles[r % len(tiles)][:, :], tiles[r % len(tiles)][:, :], x_rstd[r][:, :], None,
                                        ALU.mult).then_inc(x_scaled, 1)

            def modulate(n, u0, u, r, first=False):
                dve.wait_ge(flip_full, u0 + (u + 1))
                if not first or r > 0:
                    dve.wait_ge(xn_lo_done, n * 2 + (2 * r - 1))
                    dve.wait_ge(xn_hi_done, n * 2 + 2 * r)
                for kt in range(KT // 2):
                    op = nc.vector.tensor_scalar(y_half[0][:, kt * P:(kt + 1) * P],
                                                 flip_bank[u % 2][:, kt * P:(kt + 1) * P],
                                                 mod_now[:, kt:kt + 1], mod_now[:, KT + kt:KT + kt + 1],
                                                 ALU.mult, ALU.add)
                op.then_inc(flip_free, 1)

            def mean_squares(q, tt):
                dve.wait_ge(sq_done, q + (tt + 1))
                nc.vector.tensor_reduce(qk_ms[:, tt, :], sq[tt % 2][:, :].rearrange("p (h d) -> p h d", d=DH),
                                        AX.X, ALU.add).then_inc(qk_ms_done, 1)

            def stage_qk(q, tt):
                dve.wait_ge(qk_rstd_done, q + (tt + 1))
                nc.vector.tensor_tensor(qk_stage[:, tt, :].rearrange("p (h d) -> p h d", d=DH),
                                        proj_bank[tt % 2][:, 0:2 * P].rearrange("p (h d) -> p h d", d=DH),
                                        qk_rstd[:, tt, :].unsqueeze(2).to_broadcast([P, 4, DH]),
                                        ALU.mult).then_inc(proj_drained, 1)

            def add_residual(b, c, tt):
                g = c * TT + tt
                _, n = OUT_COLS[c]
                dve.wait_ge(proj_done, (out_job(b) + c) * TT + (tt + 1))
                dve.wait_ge(res_loaded[g % NRES], b * (16 * NOUT * TT // NRES) + 16 * (g // NRES + 1))
                nc.vector.tensor_tensor(res[g % NRES][:, 0:n], proj_bank[tt % 2][:, 0:n],
                                        res[g % NRES][:, 0:n], ALU.add).then_inc(proj_drained, 1)

            def norm_probs(it, n):
                h, i = n // 4, n % 4
                dve.wait_ge(exp_done, it * 8 + (n + 1 + CREDIT))
                nc.vector.reciprocal(row_inv[:, n:n + 1], row_sum[:, n:n + 1]).then_inc(inv_done, 1)
                dve.wait_ge(inv_done, it * 8 + (n + 1))
                nc.vector.tensor_scalar(probs[h][:, i, :], probs[h][:, i, :], row_inv[:, n:n + 1], None,
                                        ALU.mult).then_inc(probs_ready, 1)

            def pair(b, p, order, next_x=False, next_kind="qkv", out_b=None):
                it, u0, j, places = pair_no(b, p), flip_no(b, p, next_x), job_no(b, p), flip_places(order)
                for step in order["VectorE"]:
                    kind, n, pair_of = step[0].upper(), int(step[1:]), it
                    if step[0] in "fw":
                        n, pair_of = n + 4, it - 1
                    if step[0] in "oq":
                        pair_of = it - 1
                    h, i = n // 4, n % 4
                    u, u_hi = places.get(step, (0, 0))
                    if kind == "T":
                        dve.wait_ge(flip_hi, flip_hi_no(b, p) + (u_hi + 1))
                        for head in range(2):
                            mine, other = rows(head), rows(1 - head)
                            if n == 0:
                                op = nc.vector.scalar_tensor_tensor(
                                    q_split[head][other, :], flip_bank[u % 2][mine, :], gq_col[mine, :],
                                    f32(q_split[head][mine, :]), ALU.mult, ALU.subtract)
                            else:
                                op = nc.vector.scalar_tensor_tensor(
                                    k_lo[head][mine, :], flip_bank[u % 2][mine, :], gk_col[mine, :],
                                    f32(k_hi[head][mine, :]), ALU.mult, ALU.subtract)
                        op.then_inc(flip_free, 1)
                    elif kind == "B":
                        nc.vector.tensor_copy(mod_now[:, :].unsqueeze(1), mod[:, bass.ds((b + 1) % B, 1), :]
                                              ).then_inc(mod_now_done, 1)
                    elif kind == "A":
                        scale_x(b * TT + TT, n, x_tile)
                    elif kind == "X":
                        if n == 0:
                            dve.wait_ge(mod_now_done, b + 2)
                        modulate(b * TT + TT, u0, u, n)
                    elif kind == "S":
                        dve.wait_ge(score_full, it * 8 + (n + 1))
                        nc.vector.tensor_reduce(neg_max[:, n:n + 1], score_bank[n % 2][:, :], AX.X, ALU.max,
                                                negate=True).then_inc(max_done, 1)
                    elif kind == "N":
                        norm_probs(it, n)
                    elif kind == "F":
                        dve.wait_ge(flip_hi, flip_hi_no(b, p) + (u_hi + 1))
                        nc.vector.tensor_tensor(pt_lo[n % 2][:, :], flip_bank[u % 2][:, :],
                                                f32(pt_hi[n % 2][:, :]), ALU.subtract).then_inc(flip_free, 1)
                    elif kind == "O":
                        dve.wait_ge(o_part_done, pair_of * 2 + (n + 1))
                        if n == 0:
                            dve.wait_ge(o_lo_done, pair_of + 1)
                        mine = rows(n)
                        nc.vector.tensor_tensor(o_pair[mine, :], pv_bank[n][mine, :], o_part[mine, :],
                                                ALU.add).then_inc(o_sum_done, 1)
                    elif kind == "D":
                        mean_squares(it * TT + TT, n)
                    elif kind == "M":
                        if n == 0:
                            dve.wait_ge(flip_full, u0 + (places["T1"][0] + 1))
                        stage_qk(it * TT + TT, n)
                    elif kind == "L":
                        split_lo(j + 1, next_kind, 2 * n)
                    elif kind == "K":
                        split_lo(out_job(out_b) + h + 1, kind_after(h), 2 * i)
                    elif kind == "R":
                        add_residual(out_b, h, i)

            dve.sem_inc(o_sum_done, CREDIT)
            for head in range(2):
                nc.vector.memset(f32(k_lo[head][rows(1 - head), :]), 0.0)
            for kt in range(0, KT, 2):
                split_lo(0, "qkv", kt)
            for r in range(TT):
                scale_x(0, r, first_x)
            dve.wait_ge(const_loaded, 16 * 5)
            nc.vector.tensor_scalar(gq_col[:, :], gq_raw[:, :], DH ** -0.5, None, ALU.mult).then_inc(mod_step, 1)
            dve.wait_ge(mod_turned, 1)
            nc.vector.tensor_tensor(mod_t[:, :, :], pv_bank[0][:, 0:2 * KT * B].rearrange("p (c b) -> p c b", b=B),
                                    b_col[:, :].unsqueeze(2).to_broadcast([P, 2 * KT, B]),
                                    ALU.add).then_inc(mod_step, 1)
            dve.wait_ge(mod_step, 2)
            nc.vector.tensor_scalar(mod_t[:, 0:KT, :], mod_t[:, 0:KT, :], 1.0, None, ALU.add).then_inc(mod_step, 1)
            dve.wait_ge(mod_step, 3)
            by_batch = mod[:, :, :].rearrange("p b c -> p c b")
            nc.vector.tensor_tensor(by_batch[:, 0:KT, :], mod_t[:, 0:KT, :],
                                    g_col[:, :].unsqueeze(2).to_broadcast([P, KT, B]),
                                    ALU.mult).then_inc(mod_step, 1)
            nc.vector.tensor_copy(by_batch[:, KT:2 * KT, :], mod_t[:, KT:2 * KT, :]).then_inc(mod_step, 1)
            dve.wait_ge(mod_step, 5)
            nc.vector.tensor_copy(mod_now[:, :], mod[:, 0, :]).then_inc(mod_now_done, 1)
            dve.wait_ge(mod_now_done, 1)
            for r in range(TT + 1):
                if r < TT:
                    modulate(0, 0, 2 * r, r, first=True)
                else:
                    for kt in range(0, KT - 2, 2):
                        split_lo(1, "qkv", kt)
                if r > 0:
                    mean_squares(0, r - 1)
                    stage_qk(0, r - 1)
            split_lo(1, "qkv", KT - 2)
            dve.wait_ge(wo_loaded, 16)
            dve.wait_ge(ident_ready, 1)
            for kt in range(KT):
                d = wo_raw[:, kt, kt * P:(kt + 1) * P]
                op = nc.vector.tensor_tensor(d, d, ident[:, :], ALU.add)
            op.then_inc(wo_ready, 1)

            batches(dve, pair)

        @block.gpsimd
        def _(pool):
            def split_lo(j, kind, kt):
                src, n = w_source(kind, kt)
                pool.wait_ge(w_hi_done, j * KT + (kt + 1))
                nc.gpsimd.tensor_tensor(w_split[:, kt, 1, 0:n], src, f32(w_split[:, kt, 0, 0:n]),
                                        ALU.subtract).then_inc(w_lo_odd, 1)

            def rstd_x(n, r):
                pool.wait_ge(x_squared, n + (r + 1))
                nc.gpsimd.tensor_tensor(x_ms_eps[r][:, :], x_ms[r][:, :], eps_col[:, 0:1], ALU.add).then_inc(x_eps_done, 1)
                pool.wait_ge(x_eps_done, n + (r + 1))
                nc.gpsimd.tensor_tensor(x_rstd[r][:, :], x_ms_eps[r][:, :], neg_half[:, 0:1],
                                        ALU.pow).then_inc(x_rstd_done, 1)

            def rstd_qk(q, tt):
                pool.wait_ge(qk_ms_done, q + (tt + 1))
                nc.gpsimd.tensor_tensor(qk_ms_eps[:, tt, :], qk_ms[:, tt, :], eps_col[:, :], ALU.add).then_inc(qk_eps_done, 1)
                pool.wait_ge(qk_eps_done, q + (tt + 1))
                nc.gpsimd.tensor_tensor(qk_rstd[:, tt, :], qk_ms_eps[:, tt, :], neg_half[:, :],
                                        ALU.pow).then_inc(qk_rstd_done, 1)

            def xn_low(n, r):
                for half in range(2):
                    pool.wait_ge(xn_hi_done, n + (2 * r + half + 1))
                    cols = slice(4 * half, 4 * half + 4), slice(r * P, (r + 1) * P)
                    nc.gpsimd.tensor_tensor(xn_lo[:, cols[0], cols[1]],
                                            y_half[half][:, :].rearrange("p (k t) -> p k t", k=4),
                                            f32(xn_hi[:, cols[0], cols[1]]),
                                            ALU.subtract).then_inc(xn_lo_done, 1)

            def pair(b, p, order, next_x=False, next_kind="qkv", out_b=None):
                it, j = pair_no(b, p), job_no(b, p)
                for step in order["GpSimd"]:
                    kind, n = step[0].upper(), int(step[1:])
                    if kind == "V":
                        pool.wait_ge(v_hi_done, it * 2 + (n + 1))
                        nc.gpsimd.tensor_tensor(v_split[n][:, :, rows(1 - n)], v_part(p, n),
                                                f32(v_split[n][:, :, rows(n)]), ALU.subtract).then_inc(v_lo_done, 1)
                    elif kind == "A":
                        rstd_x(b * TT + TT, n)
                    elif kind == "X":
                        xn_low(b * FLIP_X + FLIP_X, n)
                    elif kind == "Q":
                        pool.wait_ge(o_hi_done, it + (0 if step[0] == "q" else 1))
                        place = bass.ds(o_place(p, step), 1)
                        nc.gpsimd.tensor_tensor(o_lo[:, place, :], o_pair[:, :].unsqueeze(1), f32(o_hi[:, place, :]),
                                                ALU.subtract).then_inc(o_lo_done, 1)
                    elif kind == "D":
                        rstd_qk(it * TT + TT, n)
                    elif kind == "L":
                        split_lo(j + 1, next_kind, 2 * n + 1)
                    elif kind == "K":
                        split_lo(out_job(out_b) + n // 4 + 1, kind_after(n // 4), 2 * (n % 4) + 1)

            pool.sem_inc(v_lo_done, CREDIT)
            pool.sem_inc(o_lo_done, 1)
            nc.gpsimd.memset(neg_half[:, :], -0.5)
            nc.gpsimd.memset(eps_col[:, :], EPS)
            nc.gpsimd.memset(ident[:, :], 0.0).then_inc(ident_zero, 1)
            pool.wait_ge(ident_zero, 1)
            nc.gpsimd.affine_select(out=ident[:, :], in_=ident[:, :], compare_op=ALU.not_equal, fill=1.0, base=0,
                                    pattern=[[-1, P]], channel_multiplier=1).then_inc(ident_ready, 1)
            pool.wait_ge(ident_ready, 1)
            for kt in range(1, KT, 2):
                split_lo(0, "qkv", kt)
            for r in range(TT):
                rstd_x(0, r)
            for r in range(TT + 1):
                if r < TT:
                    xn_low(0, r)
                else:
                    for kt in range(1, KT - 2, 2):
                        split_lo(1, "qkv", kt)
                if r > 0:
                    rstd_qk(0, r - 1)
            split_lo(1, "qkv", KT - 1)

            batches(pool, pair)

        def load_res(sp, b, g):
            c, tt = divmod(g, TT)
            c0, n = OUT_COLS[c]
            sp.wait_ge(res_stored[g % NRES], b * (16 * NOUT * TT // NRES) + 16 * (g // NRES + 1))
            sp.dma_start(res[g % NRES][:, 0:n].unsqueeze(1),
                         x_rows[bass.ds(b, 1), tt, :, c0:c0 + n].rearrange("a p d -> p a d")
                         ).then_inc(res_loaded[g % NRES], 16)

        @block.sync
        def _(sp):
            def load_pair(pair_index, after=None):
                for half in range(2):
                    if after is not None:
                        sp.wait_ge(w_lo_even, after * (KT // 2) + 2 * (half + 1))
                        sp.wait_ge(w_lo_odd, after * (KT // 2) + 2 * (half + 1))
                    kts = slice(4 * half, 4 * half + 4)
                    sp.dma_start(w_raw[:, kts, :].unsqueeze(1),
                                 w_pair[bass.ds(pair_index, 1), :, kts, :].rearrange("a p k n -> p a k n")
                                 ).then_inc(raw_loaded[half], 16)

            def load_x(nb, r):
                sp.dma_start(x_tile[r % 2][:, :].unsqueeze(1),
                             x_rows[bass.ds(nb, 1), r, :, :].rearrange("a p d -> p a d")
                             ).then_inc(x_loaded[r % 2], 16)

            def load_first_x(r):
                sp.dma_start(first_x[r], x_rows[0, r, :, :]).then_inc(x_loaded[r] if r < 2 else first_x_loaded[r - 2], 16)

            nc_const = [
                (cond_sb[:, :, :], cond_t),
                (b_col[:, :], b_emb),
                (g_col[:, :], g_norm),
                (gq_raw[0:P, :], g_q.rearrange("(p a) -> p a", a=1)),
                (gk_col[0:P, :], g_k.rearrange("(p a) -> p a", a=1)),
            ]
            for i in range(NRES):
                sp.sem_inc(res_stored[i], 16)
            for dst, src in nc_const:
                sp.dma_start(dst, src).then_inc(const_loaded, 16)
            emb_rows = w_emb.rearrange("(k p) (c n) -> k p c n", p=P, n=512)
            for kt in range(KT):
                slot, uses = emb_slot(kt)
                if uses > 1:
                    sp.wait_ge(emb_used, slot + 1)
                sp.dma_start(emb_tile[slot], emb_rows[kt]).then_inc(emb_loaded[slot], 16)
                if kt == NEMB - 1:
                    load_pair(0)
            for r in range(TT):
                load_first_x(r)
            load_pair(1, after=0)
            sp.wait_ge(emb_used, KT)
            sp.dma_start(wo_raw[:, :, :], w_out.rearrange("(k p) n -> p k n", p=P)).then_inc(wo_loaded, 16)
            load_pair(2, after=1)

            def store_out(b):
                for c, (c0, n) in enumerate(OUT_COLS):
                    for tt in range(TT):
                        g = c * TT + tt
                        if g == 0:
                            for early in range(NRES - 1):
                                load_res(sp, b, early)
                        if g + NRES - 1 < NOUT * TT:
                            load_res(sp, b, g + NRES - 1)
                        sp.wait_ge(proj_drained, (out_job(b) + c) * TT + (tt + 1))
                        sp.dma_start(out_rows[bass.ds(b, 1), tt, :, c0:c0 + n].rearrange("a p d -> p a d"),
                                     res[g % NRES][:, 0:n].unsqueeze(1)).then_inc(res_stored[g % NRES], 16)

            with sp.Fori(0, B - 1) as b:
                for r in range(TT):
                    if r == 2:
                        with sp.Fori(0, PAIRS - 2) as p:
                            load_pair((p + 3) % PAIRS, after=job_no(b, p) + 1)
                    sp.wait_ge(xn_lo_done, b * FLIP_X + (FLIP_X + 2 * (r - 2) + 2))
                    load_x(b + 1, r)
                load_pair(1, after=job_no(b, PAIRS - 2) + 1)
                store_out(b)
                load_pair(2, after=out_job(b) + NOUT)
            with sp.Fori(0, PAIRS - 3) as p:
                load_pair(p + 3, after=job_no(B - 1, p) + 1)
            store_out(B - 1)
            for i in range(NRES):
                sp.wait_ge(res_stored[i], B * 16 * NOUT * TT // NRES + 16)

def kernel(x, cond_2048, L0_cond_W_emb, L0_cond_b_emb, L0_cond_g_norm, L0_cond_W_qkv, L0_cond_g_q, L0_cond_g_k,
           L0_cond_W_out):
    import numpy as np
    import concourse.bacc as bacc
    from concourse.bass_utils import run_bass_kernel_spmd

    w = np.asarray(L0_cond_W_qkv).reshape(D, 3, PAIRS, P).transpose(2, 0, 1, 3).reshape(PAIRS, D, QKV)
    data = {
        "x": np.ascontiguousarray(x),
        "cond_t": np.ascontiguousarray(np.asarray(cond_2048).T.reshape(KT, P, B).transpose(1, 0, 2)),
        "w_emb": np.ascontiguousarray(L0_cond_W_emb),
        "b_emb": np.ascontiguousarray(np.asarray(L0_cond_b_emb).reshape(2 * KT, P).T),
        "g_norm": np.ascontiguousarray(np.asarray(L0_cond_g_norm).reshape(KT, P).T),
        "w_qkv": np.ascontiguousarray(w),
        "g_q": np.concatenate([np.asarray(L0_cond_g_q)] * 2),
        "g_k": np.concatenate([np.asarray(L0_cond_g_k)] * 2),
        "w_out": np.ascontiguousarray(L0_cond_W_out),
    }
    nc = bacc.Bacc("TRN2", target_bir_lowering=False, num_devices=1)
    args = [nc.dram_tensor(f"in_{k}", a.shape, mybir.dt.from_np(a.dtype), kind="ExternalInput").ap()
            for k, a in data.items()]
    out = nc.dram_tensor("out_0", (B, T, D), F32, kind="ExternalOutput").ap()
    cond_attention(nc, *args, out)
    r = run_bass_kernel_spmd(nc, [{f"in_{k}": a for k, a in data.items()}], core_ids=[0])
    return r.results[0]["out_0"]
```
